# Optimizing a Trainium2 kernel written in Bass

```python
import numpy as np
import jax
import jax.numpy as jnp

def _softmax(x, axis=-1):
    return jax.nn.softmax(x, axis=axis)

def _gelu(x):
    return jax.nn.gelu(x, approximate=True)

def _silu(x):
    return jax.nn.silu(x)

def _sigmoid(x):
    return jax.nn.sigmoid(x)

def _layernorm(x, axis=-1, eps=1e-05):
    m = jnp.mean(x, axis=axis, keepdims=True)
    v = jnp.var(x, axis=axis, keepdims=True)
    return (x - m) / jnp.sqrt(v + eps)

def _scatter_add(tgt, idx, src, axis=0):
    return tgt.at[idx].add(src)

def _segment_sum(src, seg, n):
    return jax.ops.segment_sum(src, seg, n)
kernel_name = 'mk_prb_d1_jaxref_r8_c3e3cb'

def setup_inputs(seed: int=0):
    np.random.seed(seed)
    _w = jnp.asarray

    def _L0_attn_setup():
        import jax, jax.numpy as jnp
        import numpy as np
        B, S, D = (4, 128, 256)
        H, G = (16, 2)
        HD = D // H

        def rotate_half(x):
            x1, x2 = (x[..., :x.shape[-1] // 2], x[..., x.shape[-1] // 2:])
            return jnp.concatenate([-x2, x1], axis=-1)
        key = jax.random.key(seed)
        ks = jax.random.split(key, 9)
        scale = 0.02
        return {'x': jax.random.normal(ks[0], (B, S, D), jnp.float32), 'wq': jax.random.normal(ks[1], (D, D), jnp.float32) * scale, 'bq': jnp.zeros((D,), jnp.float32), 'wk': jax.random.normal(ks[2], (D, G * HD), jnp.float32) * scale, 'bk': jnp.zeros((G * HD,), jnp.float32), 'wv': jax.random.normal(ks[3], (D, G * HD), jnp.float32) * scale, 'bv': jnp.zeros((G * HD,), jnp.float32), 'wo': jax.random.normal(ks[4], (D, D), jnp.float32) * scale, 'bo': jnp.zeros((D,), jnp.float32)}
    _L0_attn_in = _L0_attn_setup()

    def _L0_ffn_setup():
        import jax, jax.numpy as jnp
        import numpy as np
        B, S, D, H = (4, 256, 256, 1024)

        def fwht(x):
            orig_shape = x.shape
            n = orig_shape[-1]
            x = x.reshape(-1, n)
            h = 1
            while h < n:
                xb = x.reshape(-1, n // (2 * h), 2, h)
                a = xb[:, :, 0, :]
                b = xb[:, :, 1, :]
                x = jnp.stack([a + b, a - b], axis=2).reshape(-1, n)
                h *= 2
            scale = jnp.asarray(1.0 / np.sqrt(n), dtype=x.dtype)
            return (x * scale).reshape(orig_shape)
        key = jax.random.key(seed)
        kx, k1, k2, k3 = jax.random.split(key, 4)
        x = jax.random.normal(kx, (B, S, D), dtype=jnp.float32)
        W1 = jax.random.normal(k1, (H, D), dtype=jnp.float32) * (1.0 / np.sqrt(D))
        W2 = jax.random.normal(k2, (D, H), dtype=jnp.float32) * (1.0 / np.sqrt(H))
        W3 = jax.random.normal(k3, (H, D), dtype=jnp.float32) * (1.0 / np.sqrt(D))
        return {'x': x, 'W1': W1, 'W2': W2, 'W3': W3}
    _L0_ffn_in = _L0_ffn_setup()
    _d = {'L0_attn_x': _L0_attn_in['x'], 'L0_attn_wq': _L0_attn_in['wq'], 'L0_attn_bq': _L0_attn_in['bq'], 'L0_attn_wk': _L0_attn_in['wk'], 'L0_attn_bk': _L0_attn_in['bk'], 'L0_attn_wv': _L0_attn_in['wv'], 'L0_attn_bv': _L0_attn_in['bv'], 'L0_attn_wo': _L0_attn_in['wo'], 'L0_attn_bo': _L0_attn_in['bo'], 'L0_ffn_W1': _L0_ffn_in['W1'], 'L0_ffn_W2': _L0_ffn_in['W2'], 'L0_ffn_W3': _L0_ffn_in['W3']}
    _x0 = _d['L0_attn_x']
    _d['L0_attn_x'] = jax.random.normal(jax.random.fold_in(jax.random.key(seed), 1), (4, 1024, 256), dtype=_x0.dtype)
    del _x0
    return _d

def reference(L0_attn_x, L0_attn_wq, L0_attn_bq, L0_attn_wk, L0_attn_bk, L0_attn_wv, L0_attn_bv, L0_attn_wo, L0_attn_bo, L0_ffn_W1, L0_ffn_W2, L0_ffn_W3):

    def _L0_attn_ref(x, wq, bq, wk, bk, wv, bv, wo, bo):
        import jax, jax.numpy as jnp
        import numpy as np
        B, S, D = (4, 128, 256)
        H, G = (16, 2)
        HD = D // H

        def rotate_half(x):
            x1, x2 = (x[..., :x.shape[-1] // 2], x[..., x.shape[-1] // 2:])
            return jnp.concatenate([-x2, x1], axis=-1)
        b, s, d = x.shape
        hd = HD
        q = (x @ wq + bq).reshape(b, s, H, hd)
        k = (x @ wk + bk).reshape(b, s, G, hd)
        v = (x @ wv + bv).reshape(b, s, G, hd)
        inv_freq = 1.0 / 1250 ** (jnp.arange(0, hd, 2, dtype=jnp.float32) / hd)
        t = jnp.arange(s, dtype=jnp.float32)
        freqs = jnp.outer(t, inv_freq)
        freqs = jnp.concatenate([freqs, freqs], -1)
        sin = jnp.sin(freqs)[:, None, :]
        cos = jnp.cos(freqs)[:, None, :]
        q = q * cos + rotate_half(q) * sin
        q = q * hd ** (-0.5)
        k = k * cos + rotate_half(k) * sin
        reps = H // G
        k_exp = jnp.repeat(k, reps, axis=2)
        v_exp = jnp.repeat(v, reps, axis=2)
        scores = jnp.einsum('bqhd,bkhd->bhqk', q, k_exp) * hd ** (-0.5)
        attn = jax.nn.softmax(scores, axis=-1)
        out = jnp.einsum('bhqk,bkhd->bqhd', attn, v_exp).reshape(b, s, d)
        return out @ wo + bo

    def _L0_ffn_ref(x, W1, W2, W3):
        import jax, jax.numpy as jnp
        import numpy as np
        B, S, D, H = (4, 256, 256, 1024)

        def fwht(x):
            orig_shape = x.shape
            n = orig_shape[-1]
            x = x.reshape(-1, n)
            h = 1
            while h < n:
                xb = x.reshape(-1, n // (2 * h), 2, h)
                a = xb[:, :, 0, :]
                b = xb[:, :, 1, :]
                x = jnp.stack([a + b, a - b], axis=2).reshape(-1, n)
                h *= 2
            scale = jnp.asarray(1.0 / np.sqrt(n), dtype=x.dtype)
            return (x * scale).reshape(orig_shape)
        up_gate = jnp.einsum('bsd,hd->bsh', x, W1)
        up_lin = jnp.einsum('bsd,hd->bsh', x, W3)
        hidden = jax.nn.silu(up_gate) * up_lin
        hidden = fwht(hidden)
        out = jnp.einsum('bsh,dh->bsd', hidden, W2)
        return out
    x = L0_attn_x
    xn = _layernorm(x, axis=-1)
    x = x + _L0_attn_ref(xn, L0_attn_wq, L0_attn_bq, L0_attn_wk, L0_attn_bk, L0_attn_wv, L0_attn_bv, L0_attn_wo, L0_attn_bo) + _L0_ffn_ref(xn, L0_ffn_W1, L0_ffn_W2, L0_ffn_W3)
    return x

_drawn_inputs = setup_inputs


def setup_inputs(seed=0):
    import zlib

    import numpy as np

    out = dict(_drawn_inputs(seed))
    spreads = {'L0_attn_bq': (0.0, 0.8),
     'L0_attn_bk': (0.0, 0.8),
     'L0_attn_bv': (0.0, 0.1),
     'L0_attn_bo': (0.0, 0.1)}
    factors = {'L0_attn_wq': 8.0, 'L0_attn_wk': 8.0, 'L0_attn_wv': 8.0}
    for name, (base, spread) in spreads.items():
        noise = np.random.default_rng([zlib.crc32(name.encode()), seed]).standard_normal(out[name].shape)
        drawn = base * np.exp(spread * noise) if base else spread * noise
        out[name] = jnp.asarray(drawn.astype(out[name].dtype))
    for name, factor in factors.items():
        out[name] = (out[name] * factor).astype(out[name].dtype)
    return out
```

```python
from contextlib import ExitStack

import concourse.bass as bass
from concourse import mybir

ALU = mybir.AluOpType
ACT = mybir.ActivationFunctionType
AX = mybir.AxisListType
F32 = mybir.dt.float32
BF16 = mybir.dt.bfloat16
ds = bass.ds

P = 128
B, S, D = 4, 1024, 256
NH, NG, HD = 16, 2, 16
HID = 1024
TOK = B * S
NTILE = TOK // P
BT = 4
BLK = BT * P
NBLK = TOK // BLK
ST = S // P
DC = D // P
HC = HID // P
RQK = (NH + NG) * HD
QKV = RQK + NG * HD
QKP = 3 * P
HALF = HD // 2
EPS = 1e-5

QUAD = 4
NIT = B * NG
QB = S // 512
STEPS = QB * ST
ITSTEPS = 2 * STEPS
LEAD = 21
VW = 32
NPROD = 6
QPART = [0, 0, 0, 1, 1, 2]
KPART = [0, 1, 2, 0, 1, 0]
SROWS = NPROD * HD
MROWS = 3
SCALE = 1.0 / HD


def ring_entries(j, first, last):
    g = j + LEAD
    out = []
    if not (last and g // STEPS > 1):
        out += [("S1", g // STEPS, 2 * (g % STEPS)), ("S1", g // STEPS, 2 * (g % STEPS) + 1)]
    if g % STEPS == 10 and not (last and g // STEPS > 1):
        out.append(("MT", g // STEPS, 0))
    if g % STEPS == 2 and not (last and g // STEPS - 1 > 1):
        out.append(("MT", g // STEPS - 1, 1))
    if j % ST == 2 and not (first and j == 2):
        out.append(("OT", j // ST - 1, 0))
    if not first and j == 4:
        out += [("AT", 0, 0), ("AT", 1, 0)]
    if not first and j == 6:
        out += [("WO", 0, 0), ("WO", 1, 0)]
    return out


def lead_entries(g):
    out = [("S1", g // STEPS, 2 * (g % STEPS)), ("S1", g // STEPS, 2 * (g % STEPS) + 1)]
    if g % STEPS == 10:
        out.append(("MT", g // STEPS, 0))
    if g % STEPS == 2 and g >= STEPS:
        out.append(("MT", g // STEPS - 1, 1))
    return out


TAIL = [("OT", 3, 0), ("AT", 0, 0), ("AT", 1, 0), ("WO", 0, 0), ("WO", 1, 0)]
N_LEAD = sum(len(lead_entries(g)) for g in range(LEAD))
N_FIRST = sum(len(ring_entries(j, True, False)) for j in range(ITSTEPS))
N_IT = sum(len(ring_entries(j, False, False)) for j in range(ITSTEPS))
assert N_IT % 2 == 0


def ring_base(i):
    if isinstance(i, int) and i == 0:
        return N_LEAD
    return N_LEAD + N_FIRST + (i - 1) * N_IT


def ring_place(i, j, kind, a, b, first, last):
    n = 0
    for jj in range(j):
        n += len(ring_entries(jj, first, last))
    return ring_base(i) + n + ring_entries(j, first, last).index((kind, a, b)) + 1


def ring_parity(i, n):
    return ((N_LEAD if isinstance(i, int) and i == 0 else N_LEAD + N_FIRST) + n) % 2


def build(nc, x, wqkv, bqkv, wo, bo, w1t, w3t, w2, cos_t, sin_t, nsin_t, ident_in, out):
    x_v = x.rearrange("b (n t p) d -> (b n) p t d", t=BT, p=P)
    out_v = out.rearrange("b (t p) d -> b p t d", p=P)
    parts = nc.dram_tensor("qk_parts", [3, 3, P, TOK], BF16).ap()

    with ExitStack() as ctx:
        def sb(name, shape, dt=F32):
            return ctx.enter_context(nc.sbuf_tensor(name, shape, dt))

        def sem(name):
            return ctx.enter_context(nc.semaphore(name))

        ps = ctx.enter_context(nc.psum_tensor("ps", [P, 8, 512], F32))

        ident = sb("ident", [P, P])
        identb = sb("identb", [P, P], BF16)
        wqkv_sb = sb("wqkv_sb", [P, DC, QKV])
        wo_sb = sb("wo_sb", [P, NG, D])
        w1_sb = sb("w1_sb", [P, DC, HID])
        w3_sb = sb("w3_sb", [P, DC, HID])
        w2h = [sb(f"w2h{n}", [P, DC, HID]) for n in range(2)]
        w2t = sb("w2t", [P, HC, D])
        bqkv_sb = sb("bqkv_sb", [P, QKV])
        bo_sb = sb("bo_sb", [P, D])
        cos_sb = sb("cos_sb", [P, ST, HALF])
        sin_sb = sb("sin_sb", [P, ST, HALF])
        nsin_sb = sb("nsin_sb", [P, ST, HALF])
        npow = sb("npow", [P, BT])
        epsv = sb("epsv", [P, BT])
        zeros = sb("zeros", [P, 3, P])

        x_in = sb("x_in", [P, BT, D])
        stats = sb("stats", [P, BT, 6])
        mv = sb("mv", [P, BT, 2])
        vareps = sb("vareps", [P, BT])
        rstd = sb("rstd", [P, BT])
        xn = sb("xn", [P, BT, D])
        xnt = sb("xnt", [P, DC, BLK])
        biased = sb("biased", [P, RQK])
        rcos = sb("rcos", [P, RQK])
        rsin = sb("rsin", [P, RQK])
        roped = [sb(f"roped{t}", [P, QKP]) for t in range(BT)]
        rest = [sb(f"rest{n}", [P, QKP]) for n in range(2)]
        qkp = sb("qkp", [P, 3, 3, BLK], BF16)
        sg = [sb(f"sg{n}", [P, BLK]) for n in range(2)]
        hid = sb("hid", [P, HC, BLK])
        y = sb("y", [P, NTILE, D])
        v_all = sb("v_all", [P, NTILE, NG, VW])

        q1 = [sb(f"q1_{p}", [SROWS, QUAD, S], BF16) for p in range(2)]
        k1 = [sb(f"k1_{p}", [SROWS, S], BF16) for p in range(2)]
        q2 = [sb(f"q2_{p}", [SROWS + MROWS, QUAD, S], BF16) for p in range(2)]
        k2 = [sb(f"k2_{p}", [SROWS + MROWS, S], BF16) for p in range(2)]
        v2 = [sb(f"v2_{p}", [P, ST, VW]) for p in range(2)]
        negmax = [sb(f"negmax{p}", [P, QUAD, ST]) for p in range(2)]
        mrest = [sb(f"mrest{n}", [P, 2, ST]) for n in range(2)]
        mparts = [sb(f"mparts{p}", [P, QUAD, ST, MROWS], BF16) for p in range(2)]
        prob = [hid[:, QUAD * n:QUAD * (n + 1), :] for n in range(2)]
        osum = sg[0]
        rden = [sb(f"rden{n}", [P, 4, QUAD]) for n in range(2)]
        attn = sb("attn", [P, ST, P])
        attnt = xn[:, :, :].rearrange("p t d -> p (t d)")

        w_in = sem("w_in")
        w2_in = sem("w2_in")
        x_loaded = sem("x_loaded")
        consts_set = sem("consts_set")
        stats_part = sem("stats_part")
        stats_done = sem("stats_done")
        vareps_done = sem("vareps_done")
        rstd_done = sem("rstd_done")
        xn_done = sem("xn_done")
        ybase_done = sem("ybase_done")
        xt_done = sem("xt_done")
        xnt_a = sem("xnt_a")
        xnt_b = sem("xnt_b")
        qkv_done = sem("qkv_done")
        rope_step = sem("rope_step")
        rope_done = sem("rope_done")
        qt_done = sem("qt_done")
        part1_done = sem("part1_done")
        rest_done = sem("rest_done")
        part2_done = sem("part2_done")
        part3_done = sem("part3_done")
        parts_out = sem("parts_out")
        gate_done = sem("gate_done")
        lin_done = sem("lin_done")
        silu_done = sem("silu_done")
        hid_done = sem("hid_done")
        fwht_step = sem("fwht_step")
        w2t_done = sem("w2t_done")
        w2t_copied = sem("w2t_copied")
        down_done = sem("down_done")
        y_done = sem("y_done")

        in1 = [sem(f"in1_{p}") for p in range(2)]
        in2 = [sem(f"in2_{p}") for p in range(2)]
        ring_full = sem("ring_full")
        ring_free = sem("ring_free")
        m_part1 = sem("m_part1")
        m_rest = sem("m_rest")
        m_part2 = sem("m_part2")
        m_split = sem("m_split")
        mrows_done = sem("mrows_done")
        v2_done = sem("v2_done")
        s2_done = sem("s2_done")
        exp_done = sem("exp_done")
        pv_done = sem("pv_done")
        osum_done = sem("osum_done")
        rden_done = sem("rden_done")
        out_done = sem("out_done")

        N_W = 16 * 10
        N_IN = 16 * (NPROD + 3)

        def pair(n):
            return ps[:, 2 * n:2 * n + 2, :]

        block = ctx.enter_context(nc.Block())

        @block.sync
        def _(sp):
            def load_x(i):
                sp.dma_start(x_in[:, :, :], x_v[ds(i, 1)].rearrange("a p t d -> p (a t) d")).then_inc(x_loaded, 16)

            load_x(0)
            sp.dma_start(ident[:, :], ident_in).then_inc(w_in, 16)
            sp.dma_start(wqkv_sb[:, :, :], wqkv.rearrange("(c p) n -> p c n", p=P)).then_inc(w_in, 16)
            sp.dma_start(bqkv_sb[:, :], bqkv.partition_broadcast(P)).then_inc(w_in, 16)
            sp.dma_start(bo_sb[:, :], bo.partition_broadcast(P)).then_inc(w_in, 16)
            for t, src in ((cos_sb, cos_t), (sin_sb, sin_t), (nsin_sb, nsin_t)):
                sp.dma_start(t[:, :, :], src.rearrange("(t p) f -> p t f", p=P)).then_inc(w_in, 16)
            sp.dma_start(w1_sb[:, :, :], w1t.rearrange("(c p) n -> p c n", p=P)).then_inc(w_in, 16)
            sp.dma_start(w3_sb[:, :, :], w3t.rearrange("(c p) n -> p c n", p=P)).then_inc(w_in, 16)
            sp.dma_start(w2h[0][:, :, :], w2.rearrange("(c p) n -> p c n", p=P)).then_inc(w2_in, 16)
            sp.dma_start(wo_sb[:, :, :], wo.rearrange("(g p) n -> p g n", p=P)).then_inc(w_in, 16)

            def store_parts(i):
                sp.wait_ge(part3_done, BT * (i + 1))
                for c in range(3):
                    sp.dma_start(parts[c].rearrange("a p t -> p a t")[:, :, ds(i * BLK, BLK)],
                                 qkp[:, c, :, :]).then_inc(parts_out, 16)

            sp.wait_ge(xn_done, 1)
            sp.wait_ge(ybase_done, 1)
            load_x(1)
            with sp.Fori(0, NBLK - 2) as i:
                store_parts(i)
                sp.wait_ge(xn_done, i + 2)
                sp.wait_ge(ybase_done, i + 2)
                load_x(i + 2)
            store_parts(NBLK - 2)
            store_parts(NBLK - 1)
            sp.wait_ge(parts_out, 16 * 3 * NBLK)

            def load_quad(dst_q, dst_k, i, p, done):
                g, b = i // B, i % B
                for r in range(NPROD):
                    src = parts[QPART[r], ds(g, 1), P // 2 * p:P // 2 * (p + 1), ds(b * S, S)]
                    sp.dma_start(dst_q[p][r * HD:(r + 1) * HD, :, :],
                                 src.rearrange("a (h d) t -> d (a h) t", d=HD)).then_inc(done[p], 16)
                for r0, r1 in ((0, 3), (3, 5), (5, 6)):
                    src = parts[KPART[r0]:KPART[r1 - 1] + 1, NG, ds(g * HD, HD), ds(b * S, S)]
                    sp.dma_start(dst_k[p][r0 * HD:r1 * HD, :], src).then_inc(done[p], 16)

            def load_pass1(i, p):
                load_quad(q1, k1, i, p, in1)

            def load_pass2(i, p):
                load_quad(q2, k2, i, p, in2)

            for p in range(2):
                load_pass1(0, p)
            for p in range(2):
                load_pass2(0, p)

            def refill(i):
                for p in range(2):
                    sp.wait_ge(m_split, 2 * (2 * i + p - 1))
                    load_pass1(i, p)
                    sp.wait_ge(s2_done, 4 * STEPS * (2 * i + p - 1))
                    load_pass2(i, p)

            def store_out(b, ready):
                sp.wait_ge(ring_free, ready)
                sp.dma_start(out_v[ds(b, 1)].rearrange("a p t d -> p (a t) d"),
                             y[:, ds(b * ST, ST), :]).then_inc(out_done, 16)

            with sp.Fori(1, NIT - 2) as i:
                refill(i)
            with sp.Fori(NIT - 2, NIT) as i:
                refill(i)
                store_out(i - (NIT - 2), ring_place(i - 1, 6, "WO", 1, 0, False, False))
            store_out(B - 2, ring_place(NIT - 1, 6, "WO", 1, 0, False, True))
            n_all = ring_base(NIT - 1) + sum(len(ring_entries(j, False, True)) for j in range(ITSTEPS)) + len(TAIL)
            store_out(B - 1, n_all)
            sp.wait_ge(out_done, 16 * B)

        @block.gpsimd
        def _(pool):
            nc.gpsimd.memset(npow[:, :], -0.5).then_inc(consts_set, 1)
            nc.gpsimd.memset(epsv[:, :], EPS).then_inc(consts_set, 1)
            nc.gpsimd.memset(zeros[:, :, :], 0.0).then_inc(consts_set, 1)

            def norm_scale(i):
                pool.wait_ge(stats_done, i + 1)
                nc.gpsimd.tensor_tensor(vareps[:, :], mv[:, :, 1], epsv[:, :], ALU.add).then_inc(vareps_done, 1)
                pool.wait_ge(vareps_done, i + 1)
                nc.gpsimd.tensor_tensor(rstd[:, :], vareps[:, :], npow[:, :], ALU.pow).then_inc(rstd_done, 1)

            def residual(i):
                pool.wait_ge(x_loaded, 16 * (i + 1))
                nc.gpsimd.tensor_tensor(y[:, ds(i * BT, BT), :], x_in[:, :, :],
                                        bo_sb[:, :].unsqueeze(1).broadcast_to([P, BT, D]),
                                        ALU.add).then_inc(ybase_done, 1)

            def split(i, first, last):
                for t in range(BT):
                    pool.wait_ge(rest_done, BT * i + t + 1)
                    cols = slice(t * P, (t + 1) * P)
                    r = rest[t % 2][:, :].rearrange("p (a n) -> p a n", a=3)
                    nc.gpsimd.tensor_tensor(qkp[:, 1, :, cols], r, zeros[:, :, :], ALU.add).then_inc(part2_done, 1)
                    pool.wait_ge(part2_done, BT * i + t + 1)
                    nc.gpsimd.tensor_tensor(qkp[:, 2, :, cols], r, qkp[:, 1, :, cols],
                                            ALU.subtract).then_inc(part3_done, 1)
                if not last:
                    norm_scale(i + 1)
                    residual(i + 1)

            pool.wait_ge(w_in, N_W)
            pool.wait_ge(consts_set, 3)
            norm_scale(0)
            residual(0)
            split(0, True, False)
            with pool.Fori(1, NBLK - 1) as i:
                split(i, False, False)
            split(NBLK - 1, False, True)

            def split_max(p, k, n, free):
                pool.wait_ge(ring_free, free)
                m = negmax[p][:, 2 * k:2 * k + 2, :]
                to = mparts[p][:, 2 * k:2 * k + 2, :, :]
                nc.gpsimd.tensor_tensor(to[:, :, :, 0], m, zeros[:, 0:2, 0:ST], ALU.add).then_inc(m_part1, 1)
                pool.wait_ge(m_part1, n + 1)
                nc.gpsimd.tensor_tensor(mrest[k][:, :, :], m, to[:, :, :, 0], ALU.subtract).then_inc(m_rest, 1)
                pool.wait_ge(m_rest, n + 1)
                nc.gpsimd.tensor_tensor(to[:, :, :, 1], mrest[k][:, :, :], zeros[:, 0:2, 0:ST], ALU.add).then_inc(m_part2, 1)
                pool.wait_ge(m_part2, n + 1)
                nc.gpsimd.tensor_tensor(to[:, :, :, 2], mrest[k][:, :, :], to[:, :, :, 1],
                                        ALU.subtract).then_inc(m_split, 1)

            done = 0
            for g in range(LEAD):
                done += 2
                if g % ST == ST - 1:
                    split_max(g // STEPS, (g % STEPS) // ST, g // ST, done)
                done = done + len(lead_entries(g)) - 2

            def iteration(i, first, last):
                seen = 0
                for j in range(ITSTEPS):
                    g = j + LEAD
                    if g % ST == ST - 1 and not (last and g // STEPS > 1):
                        q = g // STEPS
                        split_max(q % 2, (g % STEPS) // ST, 4 * i + g // ST, ring_base(i) + seen + 2)
                    seen += len(ring_entries(j, first, last))

            iteration(0, True, False)
            with pool.Fori(1, NIT - 1) as i:
                iteration(i, False, False)
            iteration(NIT - 1, False, True)

        @block.scalar
        def _(act):
            def stage1(i, first, last):
                act.wait_ge(xt_done, DC * i + 1)
                nc.scalar.copy(xnt[:, 0, :], ps[:, 6, :]).then_inc(xnt_a, 1)
                for c in range(HC):
                    act.wait_ge(gate_done, HC * i + c + 1)
                    if not (first and c < 2):
                        act.wait_ge(hid_done, HC * i + c - 1)
                    nc.scalar.activation(sg[c % 2][:, :], ps[:, c % 2, :], ACT.Silu).then_inc(silu_done, 1)
                    t = c - 2
                    if 0 <= t < BT:
                        if t == 0 and not first:
                            act.wait_ge(parts_out, 16 * 3 * i)
                        act.wait_ge(qt_done, BT * i + t + 1)
                        nc.scalar.copy(qkp[:, 0, :, t * P:(t + 1) * P],
                                       ps[:, 4 + t, 0:QKP].rearrange("p (a n) -> p a n", a=3)).then_inc(part1_done, 1)
                if first:
                    for n in range(4):
                        act.wait_ge(w2t_done, n + 1)
                        nc.scalar.mul(w2t[:, 2 * n:2 * n + 2, :],
                                      ps[:, 4 + n, :].rearrange("p (c d) -> p c d", c=2),
                                      float(HID) ** -0.5).then_inc(w2t_copied, 1)

            stage1(0, True, False)
            with act.Fori(1, NBLK - 1) as i:
                stage1(i, False, False)
            stage1(NBLK - 1, False, True)

            def save_sums(i, s):
                n = (ITSTEPS // ST) * i + (s + 1) // ST
                act.wait_ge(pv_done, ITSTEPS * i + s + 1)
                if not (isinstance(n, int) and n <= 1):
                    act.wait_ge(rden_done, n - 1)
                nc.scalar.copy(osum[:, :], ps[:, 7, :]).then_inc(osum_done, 1)

            def iteration(i, first, last):
                for j in range(ITSTEPS):
                    for h in range(QUAD):
                        if h == 2 and j % ST == 0 and not (first and j == 0):
                            save_sums(i, j - 1)
                        u = QUAD * j + h
                        act.wait_ge(s2_done, QUAD * ITSTEPS * i + u + 1)
                        if h == 0 and not (first and j < 2):
                            act.wait_ge(pv_done, ITSTEPS * i + j - 1)
                        nc.scalar.activation(prob[j % 2][:, h, :], ps[:, 4 + u % 3, :], ACT.Exp,
                                             scale=SCALE).then_inc(exp_done, 1)

            iteration(0, True, False)
            with act.Fori(1, NIT - 1) as i:
                iteration(i, False, False)
            iteration(NIT - 1, False, True)
            save_sums(NIT - 1, ITSTEPS - 1)

        @block.vector
        def _(dve):
            nc.vector.memset(v_all[:, :, :, :], 0.0).then_inc(consts_set, 1)
            for t in range(BT):
                nc.vector.memset(roped[t][:, RQK:QKP], 0.0).then_inc(consts_set, 1)
            for p in range(2):
                nc.vector.memset(k2[p][SROWS:SROWS + MROWS, :], 1.0).then_inc(consts_set, 1)
            dve.wait_ge(w_in, N_W)
            nc.vector.tensor_copy(identb[:, :], ident[:, :]).then_inc(consts_set, 1)
            dve.wait_ge(consts_set, 11)
            nc.vector.memset(v_all[:, :, :, HD:HD + 1], 1.0).then_inc(consts_set, 1)
            dve.wait_ge(consts_set, 12)

            def norm_stats(i):
                dve.wait_ge(x_loaded, 16 * (i + 1))
                for t in range(BT):
                    nc.vector.bn_stats(stats[:, t, :], x_in[:, t, :]).then_inc(stats_part, 1)

            def gather_stats(i):
                for t in range(BT):
                    a = nc.vector.bn_aggr(mv[:, t, :], stats[:, t, :])
                a.then_inc(stats_done, 1)

            def normalise(i):
                dve.wait_ge(stats_done, i + 1)
                dve.wait_ge(rstd_done, i + 1)
                for t in range(BT):
                    a = nc.vector.tensor_scalar(xn[:, t, :], x_in[:, t, :], mv[:, t, 0:1], rstd[:, t:t + 1],
                                                ALU.subtract, ALU.mult)
                a.then_inc(xn_done, 1)

            def rotate(i, t):
                n = BT * i + t
                tile = ds(n, 1)
                bank = ps[:, 4 + t, :]
                dve.wait_ge(qkv_done, n + 1)
                nc.vector.tensor_tensor(biased[:, :], bank[:, 0:RQK], bqkv_sb[:, 0:RQK], ALU.add).then_inc(rope_step, 1)
                nc.vector.tensor_tensor(
                    v_all[:, tile, :, 0:HD].rearrange("p a g d -> p (a g) d"),
                    bank[:, RQK:QKV].rearrange("p (g d) -> p g d", g=NG),
                    bqkv_sb[:, RQK:QKV].rearrange("p (g d) -> p g d", g=NG), ALU.add).then_inc(rope_step, 1)
                dve.wait_ge(rope_step, 5 * n + 2)
                if not (isinstance(n, int) and n == 0):
                    dve.wait_ge(rope_done, n)
                at = ds((i % 2) * BT + t, 1)
                v = biased[:, :].rearrange("p (h s f) -> p h s f", s=2, f=HALF)
                vc = rcos[:, :].rearrange("p (h s f) -> p h s f", s=2, f=HALF)
                vs = rsin[:, :].rearrange("p (h s f) -> p h s f", s=2, f=HALF)
                nc.vector.tensor_tensor(vc, v, cos_sb[:, at, :].unsqueeze(1).broadcast_to([P, NH + NG, 2, HALF]),
                                        ALU.mult).then_inc(rope_step, 1)
                nc.vector.tensor_tensor(vs[:, :, 0, :], v[:, :, 1, :],
                                        nsin_sb[:, at, :].broadcast_to([P, NH + NG, HALF]),
                                        ALU.mult).then_inc(rope_step, 1)
                nc.vector.tensor_tensor(vs[:, :, 1, :], v[:, :, 0, :],
                                        sin_sb[:, at, :].broadcast_to([P, NH + NG, HALF]),
                                        ALU.mult).then_inc(rope_step, 1)
                dve.wait_ge(rope_step, 5 * n + 5)
                nc.vector.tensor_tensor(roped[t][:, 0:RQK], rcos[:, :], rsin[:, :], ALU.add).then_inc(rope_done, 1)

            def split_rest(i, t):
                dve.wait_ge(part1_done, BT * i + t + 1)
                if not (isinstance(i, int) and i == 0 and t < 2):
                    dve.wait_ge(part3_done, BT * i + t - 1)
                nc.vector.tensor_tensor(rest[t % 2][:, :].rearrange("p (a n) -> p a n", a=3),
                                        ps[:, 4 + t, 0:QKP].rearrange("p (a n) -> p a n", a=3),
                                        qkp[:, 0, :, t * P:(t + 1) * P], ALU.subtract).then_inc(rest_done, 1)

            def hidden(i, c):
                dve.wait_ge(silu_done, HC * i + c + 1)
                dve.wait_ge(lin_done, HC * i + c + 1)
                if c == 0 and not (isinstance(i, int) and i == 0):
                    dve.wait_ge(down_done, BT * i)
                nc.vector.tensor_tensor(hid[:, c, :], sg[c % 2][:, :], ps[:, 2 + c % 2, :], ALU.mult).then_inc(hid_done, 1)

            def transform(stage):
                h = 1 << stage
                if stage == 0:
                    dve.wait_ge(w2_in, 16)
                else:
                    dve.wait_ge(fwht_step, 2 * stage)
                a = w2h[stage % 2][:, :, :].rearrange("p c (n s h) -> p (c n) s h", s=2, h=h)
                o = w2h[(stage + 1) % 2][:, :, :].rearrange("p c (n s h) -> p (c n) s h", s=2, h=h)
                nc.vector.tensor_tensor(o[:, :, 0, :], a[:, :, 0, :], a[:, :, 1, :], ALU.add).then_inc(fwht_step, 1)
                nc.vector.tensor_tensor(o[:, :, 1, :], a[:, :, 0, :], a[:, :, 1, :], ALU.subtract).then_inc(fwht_step, 1)

            def stage1(i, first, last):
                dve.wait_ge(xt_done, DC * (i + 1))
                nc.vector.tensor_copy(xnt[:, 1, :], ps[:, 7, :]).then_inc(xnt_b, 1)
                rotate(i, 0)
                rotate(i, 1)
                stages = 0
                for c in range(HC):
                    if c == 6 and not last:
                        dve.wait_ge(stats_part, BT * (i + 2))
                    hidden(i, c)
                    if c == 6 and not last:
                        gather_stats(i + 1)
                    if c < 2:
                        rotate(i, c + 2)
                    elif c < 2 + BT:
                        split_rest(i, c - 2)
                    if first:
                        for _ in range(2 if c in (0, 7) else 1):
                            transform(stages)
                            stages += 1
                    if c == 5 and not last:
                        norm_stats(i + 1)
                if not last:
                    normalise(i + 1)
                for t in range(BT):
                    dve.wait_ge(down_done, BT * i + t + 1)
                    if t == 0:
                        dve.wait_ge(ybase_done, i + 1)
                    at = y[:, ds(BT * i + t, 1), :].rearrange("p a d -> p (a d)")
                    nc.vector.tensor_tensor(at, at, ps[:, t, 0:D], ALU.add).then_inc(y_done, 1)

            norm_stats(0)
            dve.wait_ge(stats_part, BT)
            gather_stats(0)
            normalise(0)
            stage1(0, True, False)
            with dve.Fori(1, NBLK - 1) as i:
                stage1(i, False, False)
            stage1(NBLK - 1, False, True)

            def consume(entry, i, n, slot, first):
                kind, a, b = entry
                two = pair(slot)
                dve.wait_ge(ring_full, n + 1)
                if kind == "S1":
                    h, t = b // ST, b % ST
                    if b == 0 and not (first and a < 2):
                        dve.wait_ge(m_split, 4 * i + 2 * (a - 1))
                    nc.vector.tensor_reduce(negmax[a % 2][:, h, t:t + 1], two, AX.XY, ALU.max,
                                            negate=True).then_inc(ring_free, 1)
                if kind == "MT":
                    rows = two[SROWS:SROWS + MROWS, :, :].bitcast(BF16)
                    nc.vector.tensor_copy(q2[a % 2][SROWS:SROWS + MROWS, 2 * b:2 * b + 2, :],
                                          rows).then_inc(mrows_done, 1)
                    nc.vector.engine_nop().then_inc(ring_free, 1)
                if kind == "OT":
                    q, half = (a // 2) % 2, a % 2
                    o = two[:, 0, :].rearrange("p (t h v) -> p t h v", t=4, h=QUAD)
                    nc.vector.reciprocal(rden[half][:, :, :], o[:, :, :, HD]).then_inc(rden_done, 1)
                    dve.wait_ge(rden_done, 4 * i + a + 1)
                    nc.vector.tensor_tensor(
                        attn[:, 4 * half:4 * half + 4, q * 64:(q + 1) * 64].rearrange("p t (h d) -> p t h d", h=QUAD),
                        o[:, :, :, 0:HD], rden[half][:, :, :].unsqueeze(3).broadcast_to([P, 4, QUAD, HD]),
                        ALU.mult).then_inc(ring_free, 1)
                if kind == "AT":
                    nc.vector.tensor_copy(attnt[:, a * 512:(a + 1) * 512], two[:, 0, :]).then_inc(ring_free, 1)
                if kind == "WO":
                    at = y[:, ds(((i - 1) % B) * ST + 4 * a, 4), :].rearrange("p t d -> p (t d)")
                    nc.vector.tensor_tensor(at, at, two.rearrange("p a n -> p (a n)"), ALU.add).then_inc(ring_free, 1)

            def copy_values(i, p):
                g, b = i // B, i % B
                nc.vector.tensor_scalar(
                    v2[p][:, :, :],
                    v_all[:, ds(b * ST, ST), ds(g, 1), :].rearrange("p t a v -> p (t a) v"),
                    1.0, None, ALU.mult).then_inc(v2_done, 1)

            n = 0
            copy_values(0, 0)
            for g in range(LEAD):
                for entry in lead_entries(g):
                    consume(entry, 0, n, n % 2, True)
                    n += 1

            def iteration(i, first, last):
                n = 0
                for j in range(ITSTEPS):
                    if j == ST:
                        if not first:
                            dve.wait_ge(pv_done, ITSTEPS * i)
                        copy_values(i, 1)
                    if j == 3 * ST and not last:
                        dve.wait_ge(pv_done, ITSTEPS * i + STEPS)
                        copy_values(i + 1, 0)
                    for entry in ring_entries(j, first, last):
                        consume(entry, i, ring_base(i) + n, ring_parity(i, n), first)
                        n += 1
                return n

            iteration(0, True, False)
            with dve.Fori(1, NIT - 1) as i:
                iteration(i, False, False)
            n = iteration(NIT - 1, False, True)
            for entry in TAIL:
                k = NIT - 1 if entry[0] == "OT" else NIT
                consume(entry, k, ring_base(NIT - 1) + n, ring_parity(NIT - 1, n), False)
                n += 1

        @block.tensor
        def _(pe):
            pe.wait_ge(w_in, N_W)

            def stage1(i, first, last):
                pe.wait_ge(xn_done, i + 1)
                if not first:
                    pe.wait_ge(rest_done, BT * i)
                for c in range(DC):
                    for t in range(BT):
                        a = pe.transpose(ps[:, 6 + c, t * P:(t + 1) * P], xn[:, t, c * P:(c + 1) * P], ident[:, :])
                    a.then_inc(xt_done, 1)
                pe.wait_ge(xnt_a, i + 1)
                pe.wait_ge(xnt_b, i + 1)
                for t in range(BT):
                    for c in range(DC):
                        a = pe.matmul(ps[:, 4 + t, 0:QKV], xnt[:, c, t * P:(t + 1) * P], wqkv_sb[:, c, :],
                                      start=(c == 0), stop=(c == DC - 1))
                    a.then_inc(qkv_done, 1)
                for c in range(HC):
                    if c < 2:
                        if not first:
                            pe.wait_ge(y_done, BT * i)
                    else:
                        pe.wait_ge(hid_done, HC * i + c - 1)
                    for w, bank, done in ((w1_sb, c % 2, gate_done), (w3_sb, 2 + c % 2, lin_done)):
                        for k in range(DC):
                            a = pe.matmul(ps[:, bank, :], w[:, k, c * P:(c + 1) * P], xnt[:, k, :],
                                          start=(k == 0), stop=(k == DC - 1))
                        a.then_inc(done, 1)
                    t = c - 1
                    if 0 <= t < BT:
                        pe.wait_ge(rope_done, BT * i + t + 1)
                        for k in range(3):
                            a = pe.transpose(ps[:, 4 + t, k * P:(k + 1) * P], roped[t][:, k * P:(k + 1) * P],
                                             ident[:, :])
                        a.then_inc(qt_done, 1)
                if first:
                    pe.wait_ge(fwht_step, 20)
                    pe.wait_ge(rest_done, BT)
                    for n in range(4):
                        for c in range(2):
                            for k in range(DC):
                                m = 2 * n + c
                                a = pe.transpose(ps[:, 4 + n, c * D + k * P:c * D + (k + 1) * P],
                                                 w2h[0][:, k, m * P:(m + 1) * P], ident[:, :])
                        a.then_inc(w2t_done, 1)
                    pe.wait_ge(w2t_copied, 4)
                pe.wait_ge(hid_done, HC * (i + 1))
                for t in range(BT):
                    for c in range(HC):
                        a = pe.matmul(ps[:, t, 0:D], hid[:, c, t * P:(t + 1) * P], w2t[:, c, :],
                                      start=(c == 0), stop=(c == HC - 1))
                    a.then_inc(down_done, 1)

            stage1(0, True, False)
            with pe.Fori(1, NBLK - 1) as i:
                stage1(i, False, False)
            stage1(NBLK - 1, False, True)

            pe.wait_ge(y_done, NTILE)
            pe.wait_ge(rest_done, NTILE)

            def fill(entry, i, n, slot, first):
                kind, a, b = entry
                two = pair(slot)
                if not (isinstance(n, int) and n < 2):
                    pe.wait_ge(ring_free, n - 1)
                if kind == "S1":
                    p, h, t = a % 2, b // ST, b % ST
                    if b == 0:
                        pe.wait_ge(in1[p], N_IN * (i + a // 2 + 1))
                    for e in range(2):
                        m = pe.matmul(two[:, e, :], q1[p][:, h, t * P:(t + 1) * P], k1[p][:, e * 512:(e + 1) * 512],
                                      start=True, stop=True)
                if kind == "MT":
                    pe.wait_ge(m_split, 4 * i + 2 * a + b + 1)
                    rows = two[SROWS:SROWS + MROWS, :, :].bitcast(BF16)
                    for h in range(2):
                        for t in range(ST):
                            m = pe.transpose(rows[:, h, t * P:(t + 1) * P], mparts[a % 2][:, 2 * b + h, t, :],
                                             identb[:, :])
                if kind == "OT":
                    pe.wait_ge(osum_done, 4 * i + a + 1)
                    for t in range(4):
                        m = pe.transpose(two[:, 0, t * P:(t + 1) * P], osum[:, t * P:(t + 1) * P], ident[:, :])
                if kind == "AT":
                    for t in range(4):
                        m = pe.transpose(two[:, 0, t * P:(t + 1) * P], attn[:, 4 * a + t, :], ident[:, :])
                if kind == "WO":
                    g = (i - 1) // B
                    for t in range(4):
                        m = pe.matmul(two[:, t // 2, (t % 2) * D:(t % 2 + 1) * D],
                                      attnt[:, (4 * a + t) * P:(4 * a + t + 1) * P],
                                      wo_sb[:, ds(g, 1), :].rearrange("p a n -> p (a n)"), start=True, stop=True)
                m.then_inc(ring_full, 1)

            n = 0
            for g in range(LEAD):
                for entry in lead_entries(g):
                    if entry[0] in ("AT", "WO"):
                        continue
                    fill(entry, 0, n, n % 2, True)
                    n += 1

            def scores(i, first, j, h):
                u = QUAD * j + h
                p, half, kt = j // STEPS, (j % STEPS) // ST, j % ST
                if j % STEPS == 0 and h == 0:
                    pe.wait_ge(in2[p], N_IN * (i + 1))
                    pe.wait_ge(mrows_done, 4 * i + 2 * p + 2)
                before = u - 3 if u >= 3 else {0: -2, 1: -1, 2: -3}[u]
                if not (first and before < 0):
                    pe.wait_ge(exp_done, QUAD * ITSTEPS * i + before + 1)
                pe.matmul(ps[:, 4 + u % 3, :], k2[p][:, kt * P:(kt + 1) * P], q2[p][:, h, half * 512:(half + 1) * 512],
                          start=True, stop=True).then_inc(s2_done, 1)

            def sums(i, first, s):
                p, kt = s // STEPS, s % ST
                if s % STEPS == 0:
                    pe.wait_ge(v2_done, 2 * i + p + 1)
                if kt == 0 and not (first and s == 0):
                    pe.wait_ge(osum_done, 4 * i + s // ST)
                pe.wait_ge(exp_done, QUAD * ITSTEPS * i + QUAD * (s + 1))
                for h in range(QUAD):
                    m = pe.matmul(ps[VW * h:VW * (h + 1), 7, :], v2[p][:, kt, :], prob[s % 2][:, h, :],
                                  start=(kt == 0), stop=(kt == ST - 1))
                m.then_inc(pv_done, 1)

            def iteration(i, first, last):
                n = 0
                for j in range(ITSTEPS):
                    entries = ring_entries(j, first, last)
                    scores(i, first, j, 0)
                    scores(i, first, j, 1)
                    if j > 0:
                        sums(i, first, j - 1)
                    elif not first:
                        sums(i - 1, False, ITSTEPS - 1)
                    scores(i, first, j, 2)
                    for k, entry in enumerate(entries):
                        if k == 1:
                            scores(i, first, j, 3)
                        fill(entry, i, ring_base(i) + n, ring_parity(i, n), first)
                        n += 1
                    if len(entries) < 2:
                        scores(i, first, j, 3)
                return n

            iteration(0, True, False)
            with pe.Fori(1, NIT - 1) as i:
                iteration(i, False, False)
            n = iteration(NIT - 1, False, True)
            sums(NIT - 1, False, ITSTEPS - 1)
            for entry in TAIL:
                k = NIT - 1 if entry[0] == "OT" else NIT
                fill(entry, k, ring_base(NIT - 1) + n, ring_parity(NIT - 1, n), False)
                n += 1


def kernel(**inputs):
    import numpy as np
    import concourse.bacc as bacc
    from concourse.bass_utils import run_bass_kernel_spmd

    a = {k: np.asarray(v) for k, v in inputs.items()}
    inv_freq = (1.0 / np.float32(1250) ** (np.arange(0, HD, 2, dtype=np.float32) / np.float32(HD))).astype(np.float32)
    freqs = np.outer(np.arange(S, dtype=np.float32), inv_freq).astype(np.float32)
    sin = np.sin(freqs).astype(np.float32)
    arrays = {
        "x": a["L0_attn_x"],
        "wqkv": np.concatenate([a["L0_attn_wq"], a["L0_attn_wk"], a["L0_attn_wv"]], axis=1),
        "bqkv": np.concatenate([a["L0_attn_bq"], a["L0_attn_bk"], a["L0_attn_bv"]]),
        "wo": a["L0_attn_wo"],
        "bo": a["L0_attn_bo"],
        "w1t": a["L0_ffn_W1"].T,
        "w3t": a["L0_ffn_W3"].T,
        "w2": a["L0_ffn_W2"],
        "cos_t": np.cos(freqs).astype(np.float32),
        "sin_t": sin,
        "nsin_t": -sin,
        "ident_in": np.eye(P, dtype=np.float32),
    }
    nc = bacc.Bacc("TRN2", target_bir_lowering=False, num_devices=1)
    feed, aps = {}, {}
    for name, v in arrays.items():
        v = np.ascontiguousarray(v)
        feed[f"in_{name}"] = v
        aps[name] = nc.dram_tensor(f"in_{name}", v.shape, mybir.dt.from_np(v.dtype), kind="ExternalInput").ap()
    out = nc.dram_tensor("out", (B, S, D), F32, kind="ExternalOutput").ap()
    build(nc, *aps.values(), out)
    r = run_bass_kernel_spmd(nc, [feed], core_ids=[0])
    return r.results[0]["out"]
```

```python
from contextlib import ExitStack

import concourse.bass as bass
from concourse import mybir

ALU = mybir.AluOpType
ACT = mybir.ActivationFunctionType
AX = mybir.AxisListType
F32 = mybir.dt.float32
F32R = mybir.dt.float32r
BF16 = mybir.dt.bfloat16
ds = bass.ds

P = 128
B, S, D = 4, 1024, 256
NH, NG, HD = 16, 2, 16
HID = 1024
TOK = B * S
NTILE = TOK // P
BT = 4
BLK = BT * P
NBLK = TOK // BLK
ST = S // P
DC = D // P
HC = HID // P
FWHT_STAGES = HC.bit_length() - 1
RQK = (NH + NG) * HD
QKV = RQK + NG * HD
QKP = 3 * P
HALF = HD // 2
EPS = 1e-5

QUAD = 4
NIT = B * NG
QB = S // 512
STEPS = QB * ST
ITSTEPS = 2 * STEPS
LEAD = 22
VW = 32
NPROD = 6
QPART = [0, 0, 0, 1, 1, 2]
KPART = [0, 1, 2, 0, 1, 0]
SROWS = NPROD * HD
MROWS = 3
SCALE = 1.0 / HD


def ring_entries(j, first, last):
    g = j + LEAD
    out = []
    if not (last and g // STEPS > 1):
        out += [("S1", g // STEPS, 2 * (g % STEPS)), ("S1", g // STEPS, 2 * (g % STEPS) + 1)]
    if g % STEPS == 10 and not (last and g // STEPS > 1):
        out.append(("MT", g // STEPS, 0))
    if g % STEPS == 2 and not (last and g // STEPS - 1 > 1):
        out.append(("MT", g // STEPS - 1, 1))
    if j % ST == 2 and not (first and j == 2):
        out.append(("OT", j // ST - 1, 0))
    if not first and j == 4:
        out += [("AT", 0, 0), ("AT", 1, 0)]
    if not first and j == 6:
        out += [("WO", 0, 0), ("WO", 1, 0)]
    return out


def lead_entries(g):
    out = [("S1", g // STEPS, 2 * (g % STEPS)), ("S1", g // STEPS, 2 * (g % STEPS) + 1)]
    if g % STEPS == 10:
        out.append(("MT", g // STEPS, 0))
    if g % STEPS == 2 and g >= STEPS:
        out.append(("MT", g // STEPS - 1, 1))
    return out


TAIL = [("OT", 3, 0), ("AT", 0, 0), ("AT", 1, 0), ("WO", 0, 0), ("WO", 1, 0)]
GAPS = QUAD + 1
SUMS_AT = 4

L_SCORE, L_SUMS = 512, 2200
L_FILL = {"S1": 1024, "MT": 800, "OT": 1050, "AT": 1050, "WO": 4100}
L_TAKE = {"S1": 2900, "MT": 3100, "OT": 2400, "AT": 1600, "WO": 2900}


def ring_schedule(first, last):
    todo = [(j, entry) for j in range(ITSTEPS) for entry in ring_entries(j, first, last)]
    out, now_pe, taken = [], 0, [0, 0]
    for place in range(GAPS * ITSTEPS):
        now_pe += L_SUMS if place % GAPS == SUMS_AT else L_SCORE
        now = []
        while todo and todo[0][0] - (todo[0][1][0] == "S1") <= place // GAPS and (taken[-2] <= now_pe or place == GAPS * ITSTEPS - 1):
            entry = todo.pop(0)[1]
            now.append(entry)
            now_pe += L_FILL[entry[0]]
            taken.append(max(taken[-1], now_pe) + L_TAKE[entry[0]])
            if len(now) == 1 and place < GAPS * ITSTEPS - 1:
                break
        out.append(now)
    assert not todo
    return out


N_LEAD = sum(len(lead_entries(g)) for g in range(LEAD))
N_FIRST = sum(map(len, ring_schedule(True, False)))
N_IT = sum(map(len, ring_schedule(False, False)))
N_LAST = sum(map(len, ring_schedule(False, True)))
assert N_IT % 2 == 0


def ring_base(i):
    if isinstance(i, int) and i == 0:
        return N_LEAD
    return N_LEAD + N_FIRST + (i - 1) * N_IT


def ring_place(i, entry, first, last):
    order = [e for now in ring_schedule(first, last) for e in now]
    return ring_base(i) + order.index(entry) + 1


def ring_parity(i, n):
    return ((N_LEAD if isinstance(i, int) and i == 0 else N_LEAD + N_FIRST) + n) % 2


def build(nc, x, wqkv, bqkv, wo, bo, w1t, w3t, w2t, cos_t, sin_t, nsin_t, ident_in, had_in, out):
    x_v = x.rearrange("b (n t p) d -> (b n) p t d", t=BT, p=P)
    out_v = out.rearrange("b (t p) d -> b p t d", p=P)
    parts = nc.dram_tensor("qk_parts", [3, 3, P, TOK], BF16).ap()

    with ExitStack() as ctx:
        def sb(name, shape, dt=F32):
            return ctx.enter_context(nc.sbuf_tensor(name, shape, dt))

        def sem(name):
            return ctx.enter_context(nc.semaphore(name))

        ps = ctx.enter_context(nc.psum_tensor("ps", [P, 8, 512], F32))

        ident = sb("ident", [P, P])
        had = sb("had", [P, P])
        identb = sb("identb", [P, P], BF16)
        wqkv_p = [sb(f"wqkv_p{n}", [P, DC, QKV], F32R) for n in range(2)]
        w1_p = [sb(f"w1_p{n}", [P, DC, HID], F32R) for n in range(2)]
        w3_p = [sb(f"w3_p{n}", [P, DC, HID], F32R) for n in range(2)]
        w2t_p = [sb(f"w2t_p{n}", [P, HC, D], F32R) for n in range(2)]
        w2h = [sb(f"w2h{n}", [P, HC, D]) for n in range(2)]
        wo_sb = sb("wo_sb", [P, NG, D])
        bqkv_sb = sb("bqkv_sb", [P, QKV])
        bo_sb = sb("bo_sb", [P, D])
        cos_sb = sb("cos_sb", [P, ST, HALF])
        sin_sb = sb("sin_sb", [P, ST, HALF])
        nsin_sb = sb("nsin_sb", [P, ST, HALF])
        npow = sb("npow", [P, BT])
        epsv = sb("epsv", [P, BT])
        zeros = sb("zeros", [P, 1])

        x_in = sb("x_in", [P, BT, D])
        stats = sb("stats", [P, BT, 6])
        mv = sb("mv", [P, BT, 2])
        vareps = sb("vareps", [P, BT])
        rstd = sb("rstd", [P, BT])
        xn = sb("xn", [P, BT, D])
        xnt_p = [sb(f"xnt_p{n}", [P, DC, BLK], F32R) for n in range(2)]
        work = sb("work", [P, 2 * QUAD * 512])
        cuts = [RQK, RQK, RQK, QKP, QKP, QKP, QKP, BLK, BLK]
        at = [sum(cuts[:n]) for n in range(len(cuts) + 1)]
        biased, rcos, rsin, *tiles = [work[:, a:b] for a, b in zip(at, at[1:])]
        roped, rest, sg = tiles[0:2], tiles[2:4], tiles[4:6]
        qkp = sb("qkp", [P, 3, 3, BLK], BF16)
        hid_p = [sb(f"hid_p{n}", [P, HC, BLK], F32R) for n in range(2)]
        y = sb("y", [P, NTILE, D])
        v_all = sb("v_all", [P, NTILE, NG, HD])

        q1 = [w2h[p][:, :, :].rearrange("p c d -> p (c d)").bitcast(BF16)[0:SROWS, :]
              .rearrange("p (h t) -> p h t", h=QUAD) for p in range(2)]
        k1 = [sb(f"k1_{p}", [SROWS, S], BF16) for p in range(2)]
        q2 = [qkp[:, :, :, :].rearrange("p c a t -> p (c a t)")[0:SROWS + MROWS, 0:QUAD * S]
              .rearrange("p (h t) -> p h t", h=QUAD),
              sb("q2_1", [SROWS + MROWS, QUAD, S], BF16)]
        k2 = [sb(f"k2_{p}", [SROWS + MROWS, S], BF16) for p in range(2)]
        v2 = [sb(f"v2_{p}", [P, ST, VW]) for p in range(2)]
        negmax = [sb(f"negmax{p}", [P, QUAD, ST]) for p in range(2)]
        mrest = [sb(f"mrest{n}", [P, 2, ST]) for n in range(2)]
        mparts = [sb(f"mparts{p}", [P, QUAD, ST, MROWS], BF16) for p in range(2)]
        prob = [work[:, QUAD * 512 * n:QUAD * 512 * (n + 1)].rearrange("p (h n) -> p h n", h=QUAD) for n in range(2)]
        osum = sb("osum", [P, 512])
        rden = [sb(f"rden{n}", [P, 4, QUAD]) for n in range(2)]
        attn = x_in[:, :, :].rearrange("p t (a n) -> p (t a) n", a=2)
        attnt = xn[:, :, :].rearrange("p t d -> p (t d)")

        w13_raw = y[:, NTILE // 2:NTILE, :].rearrange("p (w c h) d -> p w c (h d)", w=2, c=DC)
        wqkv_raw = y[:, 8:11, :].rearrange("p t d -> p (t d)")[:, 0:DC * QKV].rearrange("p (c n) -> p c n", c=DC)

        id_in = sem("id_in")
        qkv_in = sem("qkv_in")
        w13_in = [sem(f"w13_in{n}") for n in range(2)]
        bo_in = sem("bo_in")
        wo_in = sem("wo_in")
        identb_done = sem("identb_done")
        wqkv_hi = sem("wqkv_hi")
        wqkv_lo = sem("wqkv_lo")
        w13_hi = sem("w13_hi")
        w1_lo = sem("w1_lo")
        w3_lo = sem("w3_lo")
        w2_in = sem("w2_in")
        x_loaded = sem("x_loaded")
        consts_set = sem("consts_set")
        stats_part = sem("stats_part")
        stats_done = sem("stats_done")
        vareps_done = sem("vareps_done")
        rstd_done = sem("rstd_done")
        xn_done = sem("xn_done")
        ybase_done = sem("ybase_done")
        xt_done = sem("xt_done")
        xnt_hi = sem("xnt_hi")
        xnt_lo = sem("xnt_lo")
        qkv_done = sem("qkv_done")
        rope_step = sem("rope_step")
        rope_done = sem("rope_done")
        qt_done = sem("qt_done")
        part1_done = sem("part1_done")
        rest_done = sem("rest_done")
        part2_done = sem("part2_done")
        part3_done = sem("part3_done")
        parts_out = sem("parts_out")
        gate_done = sem("gate_done")
        lin_done = sem("lin_done")
        silu_done = sem("silu_done")
        hid_done = sem("hid_done")
        hid_hi = sem("hid_hi")
        hid_lo = sem("hid_lo")
        fwht_step = sem("fwht_step")
        w2t_done = sem("w2t_done")
        w2t_hi = sem("w2t_hi")
        w2t_lo = sem("w2t_lo")
        down_done = sem("down_done")
        y_done = sem("y_done")

        in1 = [sem(f"in1_{p}") for p in range(2)]
        in2 = [sem(f"in2_{p}") for p in range(2)]
        ring_full = sem("ring_full")
        ring_free = sem("ring_free")
        m_part1 = sem("m_part1")
        m_rest = sem("m_rest")
        m_part2 = sem("m_part2")
        m_split = sem("m_split")
        mrows_done = sem("mrows_done")
        v2_done = sem("v2_done")
        s2_done = sem("s2_done")
        exp_done = sem("exp_done")
        pv_done = sem("pv_done")
        osum_done = sem("osum_done")
        rden_done = sem("rden_done")
        out_done = sem("out_done")

        N_CONSTS = 11
        N_IN = 16 * (NPROD + 3)

        def pair(n):
            return ps[:, 2 * n:2 * n + 2, :]

        block = ctx.enter_context(nc.Block())

        @block.sync
        def _(sp):
            def load_x(i):
                sp.dma_start(x_in[:, :, :], x_v[ds(i, 1)].rearrange("a p t d -> p (a t) d")).then_inc(x_loaded, 16)

            load_x(0)
            sp.dma_start(ident[:, :], ident_in).then_inc(id_in, 16)
            for n in range(2):
                cols = slice(n * HID // 2, (n + 1) * HID // 2)
                for w, src in enumerate((w1t, w3t)):
                    sp.dma_start(w13_raw[:, w, :, cols],
                                 src.rearrange("(c p) n -> p c n", p=P)[:, :, cols]).then_inc(w13_in[n], 16)
            sp.dma_start(wo_sb[:, :, :], wo.rearrange("(g p) n -> p g n", p=P)).then_inc(wo_in, 16)

            def store_parts(i):
                sp.wait_ge(part3_done, BT * (i + 1))
                for c in range(3):
                    sp.dma_start(parts[c].rearrange("a p t -> p a t")[:, :, ds(i * BLK, BLK)],
                                 qkp[:, c, :, :]).then_inc(parts_out, 16)

            sp.wait_ge(xn_done, 1)
            sp.wait_ge(ybase_done, 1)
            load_x(1)
            with sp.Fori(0, NBLK - 2) as i:
                store_parts(i)
                sp.wait_ge(xn_done, i + 2)
                sp.wait_ge(ybase_done, i + 2)
                load_x(i + 2)
            store_parts(NBLK - 2)
            store_parts(NBLK - 1)
            sp.wait_ge(parts_out, 16 * 3 * NBLK)

            def load_quad(dst_q, dst_k, i, p, done):
                g, b = i // B, i % B
                for r in range(NPROD):
                    src = parts[QPART[r], ds(g, 1), P // 2 * p:P // 2 * (p + 1), ds(b * S, S)]
                    sp.dma_start(dst_q[p][r * HD:(r + 1) * HD, :, :],
                                 src.rearrange("a (h d) t -> d (a h) t", d=HD)).then_inc(done[p], 16)
                for r0, r1 in ((0, 3), (3, 5), (5, 6)):
                    src = parts[KPART[r0]:KPART[r1 - 1] + 1, NG, ds(g * HD, HD), ds(b * S, S)]
                    sp.dma_start(dst_k[p][r0 * HD:r1 * HD, :], src).then_inc(done[p], 16)

            def load_pass1(i, p):
                load_quad(q1, k1, i, p, in1)

            def load_pass2(i, p):
                load_quad(q2, k2, i, p, in2)

            for p in range(2):
                load_pass1(0, p)
            for p in range(2):
                load_pass2(0, p)

            def refill(i):
                for p in range(2):
                    sp.wait_ge(m_split, 2 * (2 * i + p - 1))
                    load_pass1(i, p)
                    sp.wait_ge(s2_done, 4 * STEPS * (2 * i + p - 1))
                    load_pass2(i, p)

            def store_out(b, ready):
                sp.wait_ge(ring_free, ready)
                sp.dma_start(out_v[ds(b, 1)].rearrange("a p t d -> p (a t) d"),
                             y[:, ds(b * ST, ST), :]).then_inc(out_done, 16)

            with sp.Fori(1, NIT - 2) as i:
                refill(i)
            with sp.Fori(NIT - 2, NIT) as i:
                refill(i)
                store_out(i - (NIT - 2), ring_place(i - 1, ("WO", 1, 0), False, False))
            store_out(B - 2, ring_place(NIT - 1, ("WO", 1, 0), False, True))
            store_out(B - 1, ring_base(NIT - 1) + N_LAST + len(TAIL))
            sp.wait_ge(out_done, 16 * B)

        @block.gpsimd
        def _(pool):
            nc.gpsimd.memset(k2[0][SROWS:SROWS + MROWS, :], 1.0).then_inc(consts_set, 1)
            nc.gpsimd.memset(k2[1][SROWS:SROWS + MROWS, :], 1.0).then_inc(consts_set, 1)
            pool.wait_ge(consts_set, 2)
            nc.gpsimd.memset(npow[:, :], -0.5).then_inc(consts_set, 1)
            nc.gpsimd.memset(epsv[:, :], EPS).then_inc(consts_set, 1)
            nc.gpsimd.memset(zeros[:, :], 0.0).then_inc(consts_set, 1)
            for p in range(2):
                nc.gpsimd.memset(v2[p][:, :, HD + 1:VW], 0.0).then_inc(consts_set, 1)
                nc.gpsimd.memset(v2[p][:, :, HD:HD + 1], 1.0).then_inc(consts_set, 1)
            for t in range(2):
                nc.gpsimd.memset(roped[t][:, RQK:QKP], 0.0).then_inc(consts_set, 1)

            def norm_scale(i):
                pool.wait_ge(stats_done, i + 1)
                nc.gpsimd.tensor_tensor(vareps[:, :], mv[:, :, 1], epsv[:, :], ALU.add).then_inc(vareps_done, 1)
                pool.wait_ge(vareps_done, i + 1)
                nc.gpsimd.tensor_tensor(rstd[:, :], vareps[:, :], npow[:, :], ALU.pow).then_inc(rstd_done, 1)

            def residual(i):
                pool.wait_ge(x_loaded, 16 * (i + 1))
                nc.gpsimd.tensor_tensor(y[:, ds(i * BT, BT), :], x_in[:, :, :],
                                        bo_sb[:, :].unsqueeze(1).broadcast_to([P, BT, D]),
                                        ALU.add).then_inc(ybase_done, 1)

            def split(i, first, last):
                for t in range(BT):
                    if t == 3 and not last:
                        norm_scale(i + 1)
                    pool.wait_ge(rest_done, BT * i + t + 1)
                    cols = slice(t * P, (t + 1) * P)
                    r = rest[t % 2][:, :].rearrange("p (a n) -> p a n", a=3)
                    nc.gpsimd.tensor_tensor(qkp[:, 1, :, cols], r, zeros[:, :].unsqueeze(2).broadcast_to([P, 3, P]), ALU.add).then_inc(part2_done, 1)
                    pool.wait_ge(part2_done, BT * i + t + 1)
                    nc.gpsimd.tensor_tensor(qkp[:, 2, :, cols], r, qkp[:, 1, :, cols],
                                            ALU.subtract).then_inc(part3_done, 1)
                if not last:
                    residual(i + 1)

            pool.wait_ge(consts_set, N_CONSTS)
            norm_scale(0)
            for n in range(2):
                cols = slice(n * HID // 2, (n + 1) * HID // 2)
                pool.wait_ge(w13_hi, 2 * n + 2)
                nc.gpsimd.tensor_tensor(w3_p[1][:, :, cols], w13_raw[:, 1, :, cols],
                                        w3_p[0][:, :, cols].bitcast(F32), ALU.subtract).then_inc(w3_lo, 1)
            pool.wait_ge(bo_in, 16)
            residual(0)
            split(0, True, False)
            with pool.Fori(1, NBLK - 1) as i:
                split(i, False, False)
            split(NBLK - 1, False, True)

            def split_max(p, k, n, free):
                pool.wait_ge(ring_free, free)
                m = negmax[p][:, 2 * k:2 * k + 2, :]
                to = mparts[p][:, 2 * k:2 * k + 2, :, :]
                nc.gpsimd.tensor_tensor(to[:, :, :, 0], m, zeros[:, :].unsqueeze(2).broadcast_to([P, 2, ST]), ALU.add).then_inc(m_part1, 1)
                pool.wait_ge(m_part1, n + 1)
                nc.gpsimd.tensor_tensor(mrest[k][:, :, :], m, to[:, :, :, 0], ALU.subtract).then_inc(m_rest, 1)
                pool.wait_ge(m_rest, n + 1)
                nc.gpsimd.tensor_tensor(to[:, :, :, 1], mrest[k][:, :, :], zeros[:, :].unsqueeze(2).broadcast_to([P, 2, ST]), ALU.add).then_inc(m_part2, 1)
                pool.wait_ge(m_part2, n + 1)
                nc.gpsimd.tensor_tensor(to[:, :, :, 2], mrest[k][:, :, :], to[:, :, :, 1],
                                        ALU.subtract).then_inc(m_split, 1)

            done = 0
            for g in range(LEAD):
                done += 2
                if g % ST == ST - 1:
                    split_max(g // STEPS, (g % STEPS) // ST, g // ST, done)
                done = done + len(lead_entries(g)) - 2

            def iteration(i, first, last):
                n = 0
                for now in ring_schedule(first, last):
                    for kind, q, unit in now:
                        n += 1
                        if kind == "S1" and unit % (2 * ST) == 2 * ST - 1:
                            k = unit // (2 * ST)
                            split_max(q % 2, k, 4 * i + 2 * q + k, ring_base(i) + n)

            iteration(0, True, False)
            with pool.Fori(1, NIT - 1) as i:
                iteration(i, False, False)
            iteration(NIT - 1, False, True)

        @block.scalar
        def _(act):
            act.dma_start(wqkv_raw, wqkv.rearrange("(c p) n -> p c n", p=P)).then_inc(qkv_in, 16)
            act.dma_start(bqkv_sb[:, :], bqkv.partition_broadcast(P)).then_inc(qkv_in, 16)
            for t, src in ((cos_sb, cos_t), (sin_sb, sin_t), (nsin_sb, nsin_t)):
                act.dma_start(t[:, :, :], src.rearrange("(t p) f -> p t f", p=P)).then_inc(qkv_in, 16)
            act.dma_start(bo_sb[:, :], bo.partition_broadcast(P)).then_inc(bo_in, 16)
            act.dma_start(w2h[0][:, :, :], w2t.rearrange("(c p) n -> p c n", p=P)).then_inc(w2_in, 16)
            act.dma_start(had[:, :], had_in).then_inc(w2_in, 16)

            act.wait_ge(id_in, 16)
            nc.scalar.copy(identb[:, :], ident[:, :]).then_inc(identb_done, 1)
            act.wait_ge(qkv_in, 16 * 5)
            nc.scalar.copy(wqkv_p[0][:, :, :], wqkv_raw).then_inc(wqkv_hi, 1)

            def turned_hi(i):
                for k in range(DC):
                    act.wait_ge(xt_done, DC * i + k + 1)
                    nc.scalar.copy(xnt_p[0][:, k, :], ps[:, 6 + k, :]).then_inc(xnt_hi, 1)

            def hidden_hi(i, c, first):
                act.wait_ge(hid_done, HC * i + c + 1)
                if c == 0 and not first:
                    act.wait_ge(down_done, BT * i)
                nc.scalar.copy(hid_p[0][:, c, :], sg[c % 2][:, :]).then_inc(hid_hi, 1)

            def stage1(i, first, last):
                for c in range(HC):
                    act.wait_ge(gate_done, HC * i + c + 1)
                    if not (first and c < 2):
                        act.wait_ge(hid_lo, HC * i + c - 1)
                    nc.scalar.activation(sg[c % 2][:, :], ps[:, c % 2, :], ACT.Silu).then_inc(silu_done, 1)
                    if c > 0:
                        hidden_hi(i, c - 1, first)
                    t = c - 2
                    if 0 <= t < BT:
                        if t == 0 and not first:
                            act.wait_ge(parts_out, 16 * 3 * i)
                        act.wait_ge(qt_done, BT * i + t + 1)
                        nc.scalar.copy(qkp[:, 0, :, t * P:(t + 1) * P],
                                       ps[:, 4 + t, 0:QKP].rearrange("p (a n) -> p a n", a=3)).then_inc(part1_done, 1)
                if first:
                    for n in range(4):
                        act.wait_ge(w2t_done, n + 1)
                        nc.scalar.copy(w2t_p[0][:, 2 * n:2 * n + 2, :],
                                       ps[:, 4 + n, :].rearrange("p (c d) -> p c d", c=2)).then_inc(w2t_hi, 1)
                hidden_hi(i, HC - 1, first)
                if not last:
                    turned_hi(i + 1)

            turned_hi(0)
            for n in range(2):
                cols = slice(n * HID // 2, (n + 1) * HID // 2)
                act.wait_ge(w13_in[n], 32)
                for w, to in enumerate((w1_p, w3_p)):
                    nc.scalar.copy(to[0][:, :, cols], w13_raw[:, w, :, cols]).then_inc(w13_hi, 1)
            stage1(0, True, False)
            with act.Fori(1, NBLK - 1) as i:
                stage1(i, False, False)
            stage1(NBLK - 1, False, True)

            def save_sums(i, s):
                n = (ITSTEPS // ST) * i + (s + 1) // ST
                act.wait_ge(pv_done, ITSTEPS * i + s + 1)
                if not (isinstance(n, int) and n <= 1):
                    act.wait_ge(rden_done, n - 1)
                nc.scalar.copy(osum[:, :], ps[:, 7, :]).then_inc(osum_done, 1)

            def iteration(i, first, last):
                for j in range(ITSTEPS):
                    for h in range(QUAD):
                        if h == 1 and j % ST == 1 and not (first and j == 1):
                            save_sums(i, j - 2)
                        u = QUAD * j + h
                        act.wait_ge(s2_done, QUAD * ITSTEPS * i + u + 1)
                        if h == 0 and not (first and j < 2):
                            act.wait_ge(pv_done, ITSTEPS * i + j - 1)
                        nc.scalar.activation(prob[j % 2][:, h, :], ps[:, 4 + u % 3, :], ACT.Exp,
                                             scale=SCALE).then_inc(exp_done, 1)

            iteration(0, True, False)
            with act.Fori(1, NIT - 1) as i:
                iteration(i, False, False)
            iteration(NIT - 1, False, True)
            save_sums(NIT - 1, ITSTEPS - 1)

        @block.vector
        def _(dve):
            def norm_stats(i):
                dve.wait_ge(x_loaded, 16 * (i + 1))
                for t in range(BT):
                    nc.vector.bn_stats(stats[:, t, :], x_in[:, t, :]).then_inc(stats_part, 1)

            def gather_stats(i):
                for t in range(BT):
                    a = nc.vector.bn_aggr(mv[:, t, :], stats[:, t, :])
                a.then_inc(stats_done, 1)

            def normalise(i):
                dve.wait_ge(stats_done, i + 1)
                dve.wait_ge(rstd_done, i + 1)
                for t in range(BT):
                    a = nc.vector.tensor_scalar(xn[:, t, :], x_in[:, t, :], mv[:, t, 0:1], rstd[:, t:t + 1],
                                                ALU.subtract, ALU.mult)
                a.then_inc(xn_done, 1)

            def rotate(i, t):
                n = BT * i + t
                tile = ds(n, 1)
                bank = ps[:, 4 + t, :]
                dve.wait_ge(qkv_done, n + 1)
                if not (isinstance(n, int) and n < 2):
                    dve.wait_ge(qt_done, n - 1)
                nc.vector.tensor_tensor(biased[:, :], bank[:, 0:RQK], bqkv_sb[:, 0:RQK], ALU.add).then_inc(rope_step, 1)
                nc.vector.tensor_tensor(
                    v_all[:, tile, :, :].rearrange("p a g d -> p (a g) d"),
                    bank[:, RQK:QKV].rearrange("p (g d) -> p g d", g=NG),
                    bqkv_sb[:, RQK:QKV].rearrange("p (g d) -> p g d", g=NG), ALU.add).then_inc(rope_step, 1)
                dve.wait_ge(rope_step, 5 * n + 2)
                if not (isinstance(n, int) and n == 0):
                    dve.wait_ge(rope_done, n)
                at = ds((i % 2) * BT + t, 1)
                v = biased[:, :].rearrange("p (h s f) -> p h s f", s=2, f=HALF)
                vc = rcos[:, :].rearrange("p (h s f) -> p h s f", s=2, f=HALF)
                vs = rsin[:, :].rearrange("p (h s f) -> p h s f", s=2, f=HALF)
                nc.vector.tensor_tensor(vc, v, cos_sb[:, at, :].unsqueeze(1).broadcast_to([P, NH + NG, 2, HALF]),
                                        ALU.mult).then_inc(rope_step, 1)
                nc.vector.tensor_tensor(vs[:, :, 0, :], v[:, :, 1, :],
                                        nsin_sb[:, at, :].broadcast_to([P, NH + NG, HALF]),
                                        ALU.mult).then_inc(rope_step, 1)
                nc.vector.tensor_tensor(vs[:, :, 1, :], v[:, :, 0, :],
                                        sin_sb[:, at, :].broadcast_to([P, NH + NG, HALF]),
                                        ALU.mult).then_inc(rope_step, 1)
                dve.wait_ge(rope_step, 5 * n + 5)
                nc.vector.tensor_tensor(roped[t % 2][:, 0:RQK], rcos[:, :], rsin[:, :], ALU.add).then_inc(rope_done, 1)

            def split_rest(i, t):
                dve.wait_ge(part1_done, BT * i + t + 1)
                if not (isinstance(i, int) and i == 0 and t < 2):
                    dve.wait_ge(part3_done, BT * i + t - 1)
                nc.vector.tensor_tensor(rest[t % 2][:, :].rearrange("p (a n) -> p a n", a=3),
                                        ps[:, 4 + t, 0:QKP].rearrange("p (a n) -> p a n", a=3),
                                        qkp[:, 0, :, t * P:(t + 1) * P], ALU.subtract).then_inc(rest_done, 1)

            def hidden(i, c):
                dve.wait_ge(silu_done, HC * i + c + 1)
                dve.wait_ge(lin_done, HC * i + c + 1)
                nc.vector.tensor_tensor(sg[c % 2][:, :], sg[c % 2][:, :], ps[:, 2 + c % 2, :],
                                        ALU.mult).then_inc(hid_done, 1)

            def hidden_lo(i, c):
                dve.wait_ge(hid_hi, HC * i + c + 1)
                nc.vector.tensor_tensor(hid_p[1][:, c, :], sg[c % 2][:, :], hid_p[0][:, c, :].bitcast(F32),
                                        ALU.subtract).then_inc(hid_lo, 1)

            def turned_lo(i):
                for k in range(DC):
                    dve.wait_ge(xnt_hi, DC * i + k + 1)
                    nc.vector.tensor_tensor(xnt_p[1][:, k, :], ps[:, 6 + k, :], xnt_p[0][:, k, :].bitcast(F32),
                                            ALU.subtract).then_inc(xnt_lo, 1)

            def transform(stage):
                h = 1 << stage
                if stage == 0:
                    dve.wait_ge(w2_in, 32)
                else:
                    dve.wait_ge(fwht_step, 2 * stage)
                a = w2h[stage % 2][:, :, :].rearrange("p (n s h) d -> p n s (h d)", s=2, h=h)
                o = w2h[(stage + 1) % 2][:, :, :].rearrange("p (n s h) d -> p n s (h d)", s=2, h=h)
                nc.vector.tensor_tensor(o[:, :, 0, :], a[:, :, 0, :], a[:, :, 1, :], ALU.add).then_inc(fwht_step, 1)
                nc.vector.tensor_tensor(o[:, :, 1, :], a[:, :, 0, :], a[:, :, 1, :], ALU.subtract).then_inc(fwht_step, 1)

            def stage1(i, first, last):
                rotate(i, 0)
                rotate(i, 1)
                stages = 0
                for c in range(HC):
                    if c == 3 and not last:
                        dve.wait_ge(stats_part, BT * (i + 2))
                    hidden(i, c)
                    if c == 3 and not last:
                        gather_stats(i + 1)
                    if c > 0:
                        hidden_lo(i, c - 1)
                    if c < 2:
                        rotate(i, c + 2)
                    elif c < 2 + BT:
                        split_rest(i, c - 2)
                    if first and c in (2, 4, 5):
                        transform(stages)
                        stages += 1
                    if c == 2 and not last:
                        norm_stats(i + 1)
                    if c == 6 and not last:
                        normalise(i + 1)
                if first:
                    for n in range(4):
                        dve.wait_ge(w2t_hi, n + 1)
                        nc.vector.tensor_tensor(
                            w2t_p[1][:, 2 * n:2 * n + 2, :].rearrange("p c d -> p (c d)"), ps[:, 4 + n, :],
                            w2t_p[0][:, 2 * n:2 * n + 2, :].bitcast(F32).rearrange("p c d -> p (c d)"),
                            ALU.subtract).then_inc(w2t_lo, 1)
                hidden_lo(i, HC - 1)
                if not last:
                    turned_lo(i + 1)
                for t in range(BT):
                    dve.wait_ge(down_done, BT * i + t + 1)
                    if t == 0:
                        dve.wait_ge(ybase_done, i + 1)
                    at = y[:, ds(BT * i + t, 1), :].rearrange("p a d -> p (a d)")
                    nc.vector.tensor_tensor(at, at, ps[:, t, 0:D], ALU.add).then_inc(y_done, 1)

            norm_stats(0)
            dve.wait_ge(stats_part, BT)
            gather_stats(0)
            dve.wait_ge(consts_set, N_CONSTS)
            normalise(0)
            dve.wait_ge(wqkv_hi, 1)
            nc.vector.tensor_tensor(wqkv_p[1][:, :, :], wqkv_raw, wqkv_p[0][:, :, :].bitcast(F32),
                                    ALU.subtract).then_inc(wqkv_lo, 1)
            turned_lo(0)
            for n in range(2):
                cols = slice(n * HID // 2, (n + 1) * HID // 2)
                dve.wait_ge(w13_hi, 2 * n + 1)
                nc.vector.tensor_tensor(w1_p[1][:, :, cols], w13_raw[:, 0, :, cols],
                                        w1_p[0][:, :, cols].bitcast(F32), ALU.subtract).then_inc(w1_lo, 1)
            stage1(0, True, False)
            with dve.Fori(1, NBLK - 1) as i:
                stage1(i, False, False)
            stage1(NBLK - 1, False, True)

            def consume(entry, i, n, slot, first):
                kind, a, b = entry
                two = pair(slot)
                dve.wait_ge(ring_full, n + 1)
                if kind == "S1":
                    h, t = b // ST, b % ST
                    if b == 0 and not (first and a < 2):
                        dve.wait_ge(m_split, 4 * i + 2 * (a - 1))
                    nc.vector.tensor_reduce(negmax[a % 2][:, h, t:t + 1], two, AX.XY, ALU.max,
                                            negate=True).then_inc(ring_free, 1)
                if kind == "MT":
                    rows = two[SROWS:SROWS + MROWS, :, :].bitcast(BF16)
                    nc.vector.tensor_copy(q2[a % 2][SROWS:SROWS + MROWS, 2 * b:2 * b + 2, :],
                                          rows).then_inc(mrows_done, 1)
                    nc.vector.engine_nop().then_inc(ring_free, 1)
                if kind == "OT":
                    q, half = (a // 2) % 2, a % 2
                    o = two[:, 0, :].rearrange("p (t h v) -> p t h v", t=4, h=QUAD)
                    nc.vector.reciprocal(rden[half][:, :, :], o[:, :, :, HD]).then_inc(rden_done, 1)
                    dve.wait_ge(rden_done, 4 * i + a + 1)
                    nc.vector.tensor_tensor(
                        attn[:, 4 * half:4 * half + 4, q * 64:(q + 1) * 64].rearrange("p t (h d) -> p t h d", h=QUAD),
                        o[:, :, :, 0:HD], rden[half][:, :, :].unsqueeze(3).broadcast_to([P, 4, QUAD, HD]),
                        ALU.mult).then_inc(ring_free, 1)
                if kind == "AT":
                    nc.vector.tensor_copy(attnt[:, a * 512:(a + 1) * 512], two[:, 0, :]).then_inc(ring_free, 1)
                if kind == "WO":
                    at = y[:, ds(((i - 1) % B) * ST + 4 * a, 4), :].rearrange("p t d -> p (t d)")
                    nc.vector.tensor_tensor(at, at, two.rearrange("p a n -> p (a n)"), ALU.add).then_inc(ring_free, 1)

            def copy_values(i, p):
                g, b = i // B, i % B
                nc.vector.tensor_scalar(
                    v2[p][:, :, 0:HD],
                    v_all[:, ds(b * ST, ST), ds(g, 1), :].rearrange("p t a v -> p (t a) v"),
                    1.0, None, ALU.mult).then_inc(v2_done, 1)

            n = 0
            copy_values(0, 0)
            for g in range(LEAD):
                for entry in lead_entries(g):
                    consume(entry, 0, n, n % 2, True)
                    n += 1

            def iteration(i, first, last):
                n = 0
                for now in ring_schedule(first, last):
                    for entry in now:
                        consume(entry, i, ring_base(i) + n, ring_parity(i, n), first)
                        n += 1
                        if entry[:2] == ("OT", 0):
                            if not first:
                                dve.wait_ge(pv_done, ITSTEPS * i)
                            copy_values(i, 1)
                        if entry[:2] == ("OT", 2) and not last:
                            dve.wait_ge(pv_done, ITSTEPS * i + STEPS)
                            copy_values(i + 1, 0)
                return n

            iteration(0, True, False)
            with dve.Fori(1, NIT - 1) as i:
                iteration(i, False, False)
            n = iteration(NIT - 1, False, True)
            for entry in TAIL:
                k = NIT - 1 if entry[0] == "OT" else NIT
                consume(entry, k, ring_base(NIT - 1) + n, ring_parity(NIT - 1, n), False)
                n += 1

        @block.tensor
        def _(pe):
            def product(out, left, right, first, last):
                for n, (a, b) in enumerate(((0, 0), (0, 1), (1, 0))):
                    m = pe.matmul(out, left[a], right[b], start=(first and n == 0), stop=(last and n == 2))
                return m

            def turn(i, first):
                pe.wait_ge(xn_done, i + 1)
                if not first:
                    pe.wait_ge(rest_done, BT * i)
                for c in range(DC):
                    for t in range(BT):
                        a = pe.transpose(ps[:, 6 + c, t * P:(t + 1) * P], xn[:, t, c * P:(c + 1) * P], ident[:, :])
                    a.then_inc(xt_done, 1)

            def stage1(i, first, last):
                pe.wait_ge(xnt_lo, DC * (i + 1))
                for t in range(BT):
                    for c in range(DC):
                        a = product(ps[:, 4 + t, 0:QKV], [x[:, c, t * P:(t + 1) * P] for x in xnt_p],
                                    [w[:, c, :] for w in wqkv_p], c == 0, c == DC - 1)
                    a.then_inc(qkv_done, 1)
                for c in range(HC):
                    if c < 2:
                        if not first:
                            pe.wait_ge(y_done, BT * i)
                    else:
                        pe.wait_ge(hid_done, HC * i + c - 1)
                    if first and c == HC - 1:
                        pe.wait_ge(w2_in, 32)
                        pe.wait_ge(fwht_step, 2 * FWHT_STAGES)
                        pe.wait_ge(rest_done, BT)
                        for n in range(4):
                            for m in range(2):
                                a = pe.matmul(ps[:, 4 + n, m * D:(m + 1) * D], had[:, :],
                                              w2h[FWHT_STAGES % 2][:, 2 * n + m, :], start=True, stop=True)
                            a.then_inc(w2t_done, 1)
                    if first and c % (HC // 2) == 0:
                        pe.wait_ge(w1_lo, c // (HC // 2) + 1)
                        pe.wait_ge(w3_lo, c // (HC // 2) + 1)
                    for w, bank, done in ((w1_p, c % 2, gate_done), (w3_p, 2 + c % 2, lin_done)):
                        for k in range(DC):
                            a = product(ps[:, bank, :], [v[:, k, c * P:(c + 1) * P] for v in w],
                                        [x[:, k, :] for x in xnt_p], k == 0, k == DC - 1)
                        a.then_inc(done, 1)
                    t = c - 1
                    if 0 <= t < BT:
                        pe.wait_ge(rope_done, BT * i + t + 1)
                        for k in range(3):
                            a = pe.transpose(ps[:, 4 + t, k * P:(k + 1) * P], roped[t % 2][:, k * P:(k + 1) * P],
                                             ident[:, :])
                        a.then_inc(qt_done, 1)
                if first:
                    pe.wait_ge(w2t_lo, 4)
                if not last:
                    turn(i + 1, False)
                for t in range(BT):
                    for c in range(HC):
                        if t == 0 and c in (0, HC - 1):
                            pe.wait_ge(hid_lo, HC * i + HC - (1 if c == 0 else 0))
                        a = product(ps[:, t, 0:D], [h[:, c, t * P:(t + 1) * P] for h in hid_p],
                                    [w[:, c, :] for w in w2t_p], c == 0, c == HC - 1)
                    a.then_inc(down_done, 1)

            pe.wait_ge(id_in, 16)
            turn(0, True)
            pe.wait_ge(wqkv_lo, 1)
            stage1(0, True, False)
            with pe.Fori(1, NBLK - 1) as i:
                stage1(i, False, False)
            stage1(NBLK - 1, False, True)
            pe.wait_ge(identb_done, 1)
            pe.wait_ge(wo_in, 16)

            pe.wait_ge(y_done, NTILE)
            pe.wait_ge(rest_done, NTILE)

            def fill(entry, i, n, slot, first):
                kind, a, b = entry
                two = pair(slot)
                if not (isinstance(n, int) and n < 2):
                    pe.wait_ge(ring_free, n - 1)
                if kind == "S1":
                    p, h, t = a % 2, b // ST, b % ST
                    if b == 0:
                        pe.wait_ge(in1[p], N_IN * (i + a // 2 + 1))
                    for e in range(2):
                        m = pe.matmul(two[:, e, :], q1[p][:, h, t * P:(t + 1) * P], k1[p][:, e * 512:(e + 1) * 512],
                                      start=True, stop=True)
                if kind == "MT":
                    pe.wait_ge(m_split, 4 * i + 2 * a + b + 1)
                    rows = two[SROWS:SROWS + MROWS, :, :].bitcast(BF16)
                    for h in range(2):
                        for t in range(ST):
                            m = pe.transpose(rows[:, h, t * P:(t + 1) * P], mparts[a % 2][:, 2 * b + h, t, :],
                                             identb[:, :])
                if kind == "OT":
                    pe.wait_ge(osum_done, 4 * i + a + 1)
                    for t in range(4):
                        m = pe.transpose(two[:, 0, t * P:(t + 1) * P], osum[:, t * P:(t + 1) * P], ident[:, :])
                if kind == "AT":
                    for t in range(4):
                        m = pe.transpose(two[:, 0, t * P:(t + 1) * P], attn[:, 4 * a + t, :], ident[:, :])
                if kind == "WO":
                    g = (i - 1) // B
                    for t in range(4):
                        m = pe.matmul(two[:, t // 2, (t % 2) * D:(t % 2 + 1) * D],
                                      attnt[:, (4 * a + t) * P:(4 * a + t + 1) * P],
                                      wo_sb[:, ds(g, 1), :].rearrange("p a n -> p (a n)"), start=True, stop=True)
                m.then_inc(ring_full, 1)

            n = 0
            for g in range(LEAD):
                for entry in lead_entries(g):
                    fill(entry, 0, n, n % 2, True)
                    n += 1

            def scores(i, first, j, h):
                u = QUAD * j + h
                p, half, kt = j // STEPS, (j % STEPS) // ST, j % ST
                if j % STEPS == 0 and h == 0:
                    pe.wait_ge(in2[p], N_IN * (i + 1))
                    pe.wait_ge(mrows_done, 4 * i + 2 * p + 2)
                before = u - 3 if u >= 3 else {0: -2, 1: -1, 2: -3}[u]
                if not (first and before < 0):
                    pe.wait_ge(exp_done, QUAD * ITSTEPS * i + before + 1)
                pe.matmul(ps[:, 4 + u % 3, :], k2[p][:, kt * P:(kt + 1) * P], q2[p][:, h, half * 512:(half + 1) * 512],
                          start=True, stop=True).then_inc(s2_done, 1)

            def sums(i, first, s):
                p, kt = s // STEPS, s % ST
                if s % STEPS == 0:
                    pe.wait_ge(v2_done, 2 * i + p + 1)
                if kt == 0 and not (first and s == 0):
                    pe.wait_ge(osum_done, 4 * i + s // ST)
                pe.wait_ge(exp_done, QUAD * ITSTEPS * i + QUAD * (s + 1))
                for h in range(QUAD):
                    m = pe.matmul(ps[VW * h:VW * (h + 1), 7, :], v2[p][:, kt, :], prob[s % 2][:, h, :],
                                  start=(kt == 0), stop=(kt == ST - 1))
                m.then_inc(pv_done, 1)

            def iteration(i, first, last):
                n = 0
                for place, now in enumerate(ring_schedule(first, last)):
                    j, k = place // GAPS, place % GAPS
                    if k != SUMS_AT:
                        scores(i, first, j, k if k < SUMS_AT else k - 1)
                    elif j > 0:
                        sums(i, first, j - 1)
                    elif not first:
                        sums(i - 1, False, ITSTEPS - 1)
                    for entry in now:
                        fill(entry, i, ring_base(i) + n, ring_parity(i, n), first)
                        n += 1
                return n

            iteration(0, True, False)
            with pe.Fori(1, NIT - 1) as i:
                iteration(i, False, False)
            n = iteration(NIT - 1, False, True)
            sums(NIT - 1, False, ITSTEPS - 1)
            for entry in TAIL:
                k = NIT - 1 if entry[0] == "OT" else NIT
                fill(entry, k, ring_base(NIT - 1) + n, ring_parity(NIT - 1, n), False)
                n += 1


def kernel(**inputs):
    import numpy as np
    import concourse.bacc as bacc
    from concourse.bass_utils import run_bass_kernel_spmd

    a = {k: np.asarray(v) for k, v in inputs.items()}
    inv_freq = (1.0 / np.float32(1250) ** (np.arange(0, HD, 2, dtype=np.float32) / np.float32(HD))).astype(np.float32)
    freqs = np.outer(np.arange(S, dtype=np.float32), inv_freq).astype(np.float32)
    sin = np.sin(freqs).astype(np.float32)
    hadamard = np.ones((1, 1))
    while hadamard.shape[0] < P:
        hadamard = np.kron(np.array([[1, 1], [1, -1]]), hadamard)
    hadamard = hadamard / np.sqrt(HID)
    arrays = {
        "x": a["L0_attn_x"],
        "wqkv": np.concatenate([a["L0_attn_wq"], a["L0_attn_wk"], a["L0_attn_wv"]], axis=1),
        "bqkv": np.concatenate([a["L0_attn_bq"], a["L0_attn_bk"], a["L0_attn_bv"]]),
        "wo": a["L0_attn_wo"],
        "bo": a["L0_attn_bo"],
        "w1t": a["L0_ffn_W1"].T,
        "w3t": a["L0_ffn_W3"].T,
        "w2t": a["L0_ffn_W2"].T,
        "cos_t": np.cos(freqs).astype(np.float32),
        "sin_t": sin,
        "nsin_t": -sin,
        "ident_in": np.eye(P, dtype=np.float32),
        "had_in": hadamard.astype(np.float32),
    }
    nc = bacc.Bacc("TRN2", target_bir_lowering=False, num_devices=1)
    feed, aps = {}, {}
    for name, v in arrays.items():
        v = np.ascontiguousarray(v)
        feed[f"in_{name}"] = v
        aps[name] = nc.dram_tensor(f"in_{name}", v.shape, mybir.dt.from_np(v.dtype), kind="ExternalInput").ap()
    out = nc.dram_tensor("out", (B, S, D), F32, kind="ExternalOutput").ap()
    build(nc, *aps.values(), out)
    r = run_bass_kernel_spmd(nc, [feed], core_ids=[0])
    return r.results[0]["out"]
```

```python
from contextlib import ExitStack

import concourse.bass as bass
from concourse import mybir

ALU = mybir.AluOpType
ACT = mybir.ActivationFunctionType
AX = mybir.AxisListType
F32 = mybir.dt.float32
F32R = mybir.dt.float32r
BF16 = mybir.dt.bfloat16
ds = bass.ds

P = 128
B, S, D = 4, 1024, 256
NH, NG, HD = 16, 2, 16
HID = 1024
TOK = B * S
NTILE = TOK // P
BT = 4
BLK = BT * P
NBLK = TOK // BLK
ST = S // P
DC = D // P
HC = HID // P
FWHT_STAGES = HC.bit_length() - 1
RQK = (NH + NG) * HD
QKV = RQK + NG * HD
QKP = 3 * P
HALF = HD // 2
EPS = 1e-5

QUAD = 4
NIT = B * NG
QB = S // 512
STEPS = QB * ST
ITSTEPS = 2 * STEPS
MT_AT = 1
RECIP_AT = 4
NORM_AT = (2, 7)
LEAD = 20
VW = 32
NPROD = 6
QPART = [0, 0, 0, 1, 1, 2]
KPART = [0, 1, 2, 0, 1, 0]
SROWS = NPROD * HD
MROWS = 3
SCALE = 1.0 / HD


def ring_entries(j, first, last):
    g = j + LEAD
    out = []
    if not (last and g // STEPS > 1):
        out += [("S1", g // STEPS, 2 * (g % STEPS)), ("S1", g // STEPS, 2 * (g % STEPS) + 1)]
    if g % STEPS == MT_AT and not (last and g // STEPS - 1 > 1):
        out.append(("MT", g // STEPS - 1, 0))
    if j == 2:
        out.append(("CV", 1, 0))
    if j % ST == RECIP_AT and not (first and j == RECIP_AT):
        out.append(("RC", (j // ST - 1) % 4, 0))
    if j == STEPS + 2 and not last:
        out.append(("CV", 0, 0))
    for half, step in enumerate(NORM_AT):
        if not first and j == step:
            out += [("NM", half, 0)]
        if not first and j == step + 2:
            out += [("WO", half, 0)]
    return out


def lead_entries(g):
    out = [("S1", g // STEPS, 2 * (g % STEPS)), ("S1", g // STEPS, 2 * (g % STEPS) + 1)]
    if g % STEPS == MT_AT and g >= STEPS:
        out.append(("MT", g // STEPS - 1, 0))
    return out


TAIL = [("NM", 0, 0), ("WO", 0, 0), ("RC", 3, 0), ("NM", 1, 0), ("WO", 1, 0)]
RING = ("S1", "MT", "WO")
GAPS = QUAD + 1
SUMS_AT = 4

L_SCORE, L_SUMS = 512, 2200
L_FILL = {"S1": 1024, "MT": 200, "WO": 4100}
L_TAKE = {"S1": 2800, "MT": 600, "WO": 2900, "CV": 400, "RC": 500}


def ring_schedule(first, last):
    todo = [(j, entry) for j in range(ITSTEPS) for entry in ring_entries(j, first, last)]
    out, now_pe, taken = [], 0, [0, 0]
    for place in range(GAPS * ITSTEPS):
        now_pe += L_SUMS if place % GAPS == SUMS_AT else L_SCORE
        now = []
        while todo and todo[0][0] - (todo[0][1][0] == "S1") <= place // GAPS and (taken[-2] <= now_pe or place == GAPS * ITSTEPS - 1):
            entry = todo.pop(0)[1]
            now.append(entry)
            if entry[0] not in RING:
                taken[-1] += L_TAKE.get(entry[0], 0)
                continue
            now_pe += L_FILL[entry[0]]
            taken.append(max(taken[-1], now_pe) + L_TAKE[entry[0]])
            if place < GAPS * ITSTEPS - 1:
                break
        out.append(now)
    assert not todo
    return out


def ring_length(schedule):
    return sum(entry[0] in RING for now in schedule for entry in now)


N_LEAD = sum(len(lead_entries(g)) for g in range(LEAD))
N_FIRST = ring_length(ring_schedule(True, False))
N_IT = ring_length(ring_schedule(False, False))
N_LAST = ring_length(ring_schedule(False, True))
N_TAIL = ring_length([TAIL])
assert N_IT % 2 == 0


def projected_first():
    for last in (False, True):
        for half in range(QB):
            place = [n for n, now in enumerate(ring_schedule(False, last)) if ("WO", half, 0) in now][0]
            if place >= GAPS * ST * (half + 1) + SUMS_AT:
                return False
    return True


assert projected_first()


def ring_base(i):
    if isinstance(i, int) and i == 0:
        return N_LEAD
    return N_LEAD + N_FIRST + (i - 1) * N_IT


def ring_place(i, entry, first, last):
    order = [e for now in ring_schedule(first, last) for e in now if e[0] in RING]
    return ring_base(i) + order.index(entry) + 1


def ring_parity(i, n):
    return ((N_LEAD if isinstance(i, int) and i == 0 else N_LEAD + N_FIRST) + n) % 2


def build(nc, x, wqkv, bqkv, wo, bo, w1t, w3t, w2t, cos_t, sin_t, nsin_t, ident_in, had_in, out):
    x_v = x.rearrange("b (n t p) d -> (b n) p t d", t=BT, p=P)
    out_v = out.rearrange("b (t p) d -> b p t d", p=P)
    parts = nc.dram_tensor("qk_parts", [3, 3, P, TOK], BF16).ap()
    recip_rows = nc.dram_tensor("recip_rows", [QUAD, 512], F32).ap()

    with ExitStack() as ctx:
        def sb(name, shape, dt=F32):
            return ctx.enter_context(nc.sbuf_tensor(name, shape, dt))

        def sem(name):
            return ctx.enter_context(nc.semaphore(name))

        ps = ctx.enter_context(nc.psum_tensor("ps", [P, 8, 512], F32))

        ident = sb("ident", [P, P])
        had = sb("had", [P, P])
        identb = sb("identb", [P, P], BF16)
        wqkv_p = [sb(f"wqkv_p{n}", [P, DC, QKV], F32R) for n in range(2)]
        w1_p = [sb(f"w1_p{n}", [P, DC, HID], F32R) for n in range(2)]
        w3_p = [sb(f"w3_p{n}", [P, DC, HID], F32R) for n in range(2)]
        w2t_p = [sb(f"w2t_p{n}", [P, HC, D], F32R) for n in range(2)]
        w2h = [sb(f"w2h{n}", [P, HC, D]) for n in range(2)]
        wo_sb = sb("wo_sb", [P, NG, D])
        bqkv_sb = sb("bqkv_sb", [P, QKV])
        bo_sb = sb("bo_sb", [P, D])
        cos_sb = sb("cos_sb", [P, ST, HALF])
        sin_sb = sb("sin_sb", [P, ST, HALF])
        nsin_sb = sb("nsin_sb", [P, ST, HALF])
        npow = sb("npow", [P, BT])
        epsv = sb("epsv", [P, BT])
        zeros = sb("zeros", [P, 1])

        x_in = sb("x_in", [P, BT, D])
        stats = sb("stats", [P, BT, 6])
        mv = sb("mv", [P, BT, 2])
        vareps = sb("vareps", [P, BT])
        rstd = sb("rstd", [P, BT])
        xn = sb("xn", [P, BT, D])
        xnt_p = [sb(f"xnt_p{n}", [P, DC, BLK], F32R) for n in range(2)]
        work = sb("work", [P, 2 * QUAD * 512])
        cuts = [RQK, RQK, RQK, QKP, QKP, QKP, QKP, BLK, BLK]
        at = [sum(cuts[:n]) for n in range(len(cuts) + 1)]
        biased, rcos, rsin, *tiles = [work[:, a:b] for a, b in zip(at, at[1:])]
        roped, rest, sg = tiles[0:2], tiles[2:4], tiles[4:6]
        qkp = sb("qkp", [P, 3, 3, BLK], BF16)
        hid_p = [sb(f"hid_p{n}", [P, HC, BLK], F32R) for n in range(2)]
        y = sb("y", [P, NTILE, D])
        v_all = sb("v_all", [P, NTILE, NG, HD])

        q1 = [w2h[p][:, :, :].rearrange("p c d -> p (c d)").bitcast(BF16)[0:SROWS, :]
              .rearrange("p (h t) -> p h t", h=QUAD) for p in range(2)]
        k1 = [sb(f"k1_{p}", [SROWS, S], BF16) for p in range(2)]
        q2 = [qkp[:, :, :, :].rearrange("p c a t -> p (c a t)")[0:SROWS + MROWS, 0:QUAD * S]
              .rearrange("p (h t) -> p h t", h=QUAD),
              sb("q2_1", [SROWS + MROWS, QUAD, S], BF16)]
        k2 = [sb(f"k2_{p}", [SROWS + MROWS, S], BF16) for p in range(2)]
        v2 = [sb(f"v2_{p}", [P, ST, VW]) for p in range(2)]
        negmax = [sb(f"negmax{p}", [P, QUAD, ST]) for p in range(2)]
        mrest = [sb(f"mrest{n}", [P, 2, ST]) for n in range(2)]
        mparts = [sb(f"mparts{p}", [P, MROWS, QUAD, ST], BF16) for p in range(2)]
        mturned = [sb(f"mturned{p}", [MROWS * QUAD * ST, P], BF16) for p in range(2)]
        prob = [work[:, QUAD * 512 * n:QUAD * 512 * (n + 1)].rearrange("p (h n) -> p h n", h=QUAD) for n in range(2)]
        osum = sb("osum", [P, 512])
        dens = sb("dens", [QUAD * HD, 512 // HD])
        attnt = x_in[:, :, :].rearrange("p (h t) n -> p h (t n)", h=QB)
        recips = xn[:, :, :].rearrange("p (h t) n -> p h (t n)", h=QB)

        w13_raw = y[:, NTILE // 2:NTILE, :].rearrange("p (w c h) d -> p w c (h d)", w=2, c=DC)
        wqkv_raw = y[:, 8:11, :].rearrange("p t d -> p (t d)")[:, 0:DC * QKV].rearrange("p (c n) -> p c n", c=DC)

        id_in = sem("id_in")
        wqkv_in = sem("wqkv_in")
        tables_in = sem("tables_in")
        w13_in = [sem(f"w13_in{n}") for n in range(2)]
        bo_in = sem("bo_in")
        wo_in = sem("wo_in")
        identb_done = sem("identb_done")
        wqkv_hi = sem("wqkv_hi")
        wqkv_lo = sem("wqkv_lo")
        w13_hi = sem("w13_hi")
        w1_lo = sem("w1_lo")
        w3_lo = sem("w3_lo")
        w2_in = sem("w2_in")
        x_loaded = sem("x_loaded")
        consts_set = sem("consts_set")
        stats_part = sem("stats_part")
        stats_done = sem("stats_done")
        vareps_done = sem("vareps_done")
        rstd_done = sem("rstd_done")
        xn_done = sem("xn_done")
        ybase_done = sem("ybase_done")
        xt_done = sem("xt_done")
        xnt_hi = sem("xnt_hi")
        xnt_lo = sem("xnt_lo")
        qkv_done = sem("qkv_done")
        rope_step = sem("rope_step")
        rope_done = sem("rope_done")
        qt_done = sem("qt_done")
        part1_done = sem("part1_done")
        rest_done = sem("rest_done")
        part2_done = sem("part2_done")
        part3_done = sem("part3_done")
        parts_out = sem("parts_out")
        gate_done = sem("gate_done")
        lin_done = sem("lin_done")
        silu_done = sem("silu_done")
        hid_done = sem("hid_done")
        hid_hi = sem("hid_hi")
        hid_lo = sem("hid_lo")
        fwht_step = sem("fwht_step")
        w2t_done = sem("w2t_done")
        w2t_hi = sem("w2t_hi")
        w2t_lo = sem("w2t_lo")
        down_done = sem("down_done")
        y_done = sem("y_done")

        in1 = [sem(f"in1_{p}") for p in range(2)]
        in2 = [sem(f"in2_{p}") for p in range(2)]
        ring_full = sem("ring_full")
        ring_free = sem("ring_free")
        m_part1 = sem("m_part1")
        m_rest = sem("m_rest")
        m_part2 = sem("m_part2")
        m_split = sem("m_split")
        mturned_done = sem("mturned_done")
        mrows_in = [sem(f"mrows_in{p}") for p in range(2)]
        v2_done = sem("v2_done")
        s2_done = sem("s2_done")
        exp_done = sem("exp_done")
        pv_done = sem("pv_done")
        osum_done = sem("osum_done")
        moved = [sem(f"moved{h}") for h in range(QB)]
        dens_in = sem("dens_in")
        recip_done = sem("recip_done")
        recip_out = sem("recip_out")
        norm_done = sem("norm_done")
        out_done = sem("out_done")

        N_CONSTS = 9
        N_MOVE = 16 * 2 * QUAD
        N_IN = 16 * (NPROD + 3)

        def pair(n):
            return ps[:, 2 * n:2 * n + 2, :]

        def transform(engine, vec, stage):
            h = 1 << stage
            if stage == 0:
                engine.wait_ge(w2_in, 32)
            else:
                engine.wait_ge(fwht_step, 2 * stage)
            a = w2h[stage % 2][:, :, :].rearrange("p (n s h) d -> p n s (h d)", s=2, h=h)
            o = w2h[(stage + 1) % 2][:, :, :].rearrange("p (n s h) d -> p n s (h d)", s=2, h=h)
            vec.tensor_tensor(o[:, :, 0, :], a[:, :, 0, :], a[:, :, 1, :], ALU.add).then_inc(fwht_step, 1)
            vec.tensor_tensor(o[:, :, 1, :], a[:, :, 0, :], a[:, :, 1, :], ALU.subtract).then_inc(fwht_step, 1)

        def turned_maxima(two):
            return two[0:MROWS * QUAD * ST, 0, :].bitcast(BF16)[:, 0:P]

        block = ctx.enter_context(nc.Block())

        @block.sync
        def _(sp):
            def load_x(i):
                sp.dma_start(x_in[:, :, :], x_v[ds(i, 1)].rearrange("a p t d -> p (a t) d")).then_inc(x_loaded, 16)

            load_x(0)
            sp.dma_start(ident[:, :], ident_in).then_inc(id_in, 16)
            for n in range(2):
                cols = slice(n * HID // 2, (n + 1) * HID // 2)
                for w, src in enumerate((w1t, w3t)):
                    sp.dma_start(w13_raw[:, w, :, cols],
                                 src.rearrange("(c p) n -> p c n", p=P)[:, :, cols]).then_inc(w13_in[n], 16)
            sp.dma_start(wo_sb[:, :, :], wo.rearrange("(g p) n -> p g n", p=P)).then_inc(wo_in, 16)

            def store_parts(i):
                sp.wait_ge(part3_done, BT * (i + 1))
                for c in range(3):
                    sp.dma_start(parts[c].rearrange("a p t -> p a t")[:, :, ds(i * BLK, BLK)],
                                 qkp[:, c, :, :]).then_inc(parts_out, 16)

            sp.wait_ge(xn_done, 1)
            sp.wait_ge(ybase_done, 1)
            load_x(1)
            with sp.Fori(0, NBLK - 2) as i:
                store_parts(i)
                sp.wait_ge(xn_done, i + 2)
                sp.wait_ge(ybase_done, i + 2)
                load_x(i + 2)
            store_parts(NBLK - 2)
            store_parts(NBLK - 1)
            sp.wait_ge(parts_out, 16 * 3 * NBLK)

            def load_quad(dst_q, dst_k, i, p, done):
                g, b = i // B, i % B
                for r in range(NPROD):
                    src = parts[QPART[r], ds(g, 1), P // 2 * p:P // 2 * (p + 1), ds(b * S, S)]
                    sp.dma_start(dst_q[p][r * HD:(r + 1) * HD, :, :],
                                 src.rearrange("a (h d) t -> d (a h) t", d=HD)).then_inc(done[p], 16)
                for r0, r1 in ((0, 3), (3, 5), (5, 6)):
                    src = parts[KPART[r0]:KPART[r1 - 1] + 1, NG, ds(g * HD, HD), ds(b * S, S)]
                    sp.dma_start(dst_k[p][r0 * HD:r1 * HD, :], src).then_inc(done[p], 16)

            def load_pass1(i, p):
                load_quad(q1, k1, i, p, in1)

            def load_pass2(i, p):
                load_quad(q2, k2, i, p, in2)

            for p in range(2):
                load_pass1(0, p)
            for p in range(2):
                load_pass2(0, p)

            def place_maxima(i, p):
                sp.wait_ge(mturned_done, 2 * i + p + 1)
                for c in range(MROWS):
                    sp.dma_start(q2[p][SROWS + c:SROWS + c + 1, :, :].rearrange("a h (t n) -> a (h t) n", n=P),
                                 mturned[p][c * QUAD * ST:(c + 1) * QUAD * ST, :]).then_inc(mrows_in[p], 16)

            def move_sums(i, k):
                quad, half = k // QB, k % QB
                sp.wait_ge(osum_done, 4 * i + k + 1)
                for h in range(QUAD):
                    sp.dma_start(dens[HD * h:HD * (h + 1), :],
                                 osum[VW * h + HD:VW * h + HD + 1, :].rearrange("a (g n) -> a g n", g=HD)
                                 ).then_inc(dens_in, 16)
                for h in range(QUAD):
                    to = (quad * QUAD + h) * HD
                    sp.dma_start(attnt[to:to + HD, half, :], osum[VW * h:VW * h + HD, :]).then_inc(moved[half], 16)
                sp.wait_ge(recip_done, 4 * i + k + 1)
                sp.dma_start(recip_rows.rearrange("h (g n) -> (h g) n", g=HD), dens[:, :]).then_inc(recip_out, 16)
                sp.wait_ge(recip_out, 16 * (4 * i + k + 1))
                for h in range(QUAD):
                    to = (quad * QUAD + h) * HD
                    sp.dma_start(recips[to:to + HD, half, :],
                                 recip_rows[h].partition_broadcast(HD)).then_inc(moved[half], 16)

            def refill(i):
                sp.wait_ge(m_split, 4 * i + 2)
                load_pass1(i + 1, 0)
                move_sums(i, 0)
                place_maxima(i, 1)
                sp.wait_ge(m_split, 4 * i + 4)
                load_pass1(i + 1, 1)
                sp.wait_ge(s2_done, 4 * STEPS * (2 * i + 1))
                load_pass2(i + 1, 0)
                move_sums(i, 1)
                move_sums(i, 2)
                place_maxima(i + 1, 0)
                sp.wait_ge(s2_done, 4 * STEPS * (2 * i + 2))
                load_pass2(i + 1, 1)
                move_sums(i, 3)

            def store_out(b, ready):
                sp.wait_ge(ring_free, ready)
                sp.dma_start(out_v[ds(b, 1)].rearrange("a p t d -> p (a t) d"),
                             y[:, ds(b * ST, ST), :]).then_inc(out_done, 16)

            place_maxima(0, 0)
            refill(0)
            with sp.Fori(1, NIT - 3) as i:
                refill(i)
            with sp.Fori(NIT - 3, NIT - 1) as i:
                refill(i)
                store_out(i - (NIT - 3), ring_place(i, ("WO", 1, 0), False, False))
            move_sums(NIT - 1, 0)
            place_maxima(NIT - 1, 1)
            store_out(B - 2, ring_place(NIT - 1, ("WO", 1, 0), False, True))
            for k in range(1, 4):
                move_sums(NIT - 1, k)
            for half in range(QB):
                sp.wait_ge(ring_free, ring_base(NIT - 1) + N_LAST + half + 1)
                cols = slice(half * ST // QB, (half + 1) * ST // QB)
                sp.dma_start(out_v[B - 1][:, cols, :],
                             y[:, (B - 1) * ST + half * ST // QB:(B - 1) * ST + (half + 1) * ST // QB, :]
                             ).then_inc(out_done, 16)
            sp.wait_ge(out_done, 16 * (B + 1))

        @block.gpsimd
        def _(pool):
            nc.gpsimd.memset(k2[0][SROWS:SROWS + MROWS, :], 1.0).then_inc(consts_set, 1)
            nc.gpsimd.memset(k2[1][SROWS:SROWS + MROWS, :], 1.0).then_inc(consts_set, 1)
            pool.wait_ge(consts_set, 2)
            nc.gpsimd.memset(npow[:, :], -0.5).then_inc(consts_set, 1)
            nc.gpsimd.memset(epsv[:, :], EPS).then_inc(consts_set, 1)
            nc.gpsimd.memset(zeros[:, :], 0.0).then_inc(consts_set, 1)
            for p in range(2):
                nc.gpsimd.memset(v2[p][:, :, HD:VW], 1.0).then_inc(consts_set, 1)
            for t in range(2):
                nc.gpsimd.memset(roped[t][:, RQK:QKP], 0.0).then_inc(consts_set, 1)

            def norm_scale(i):
                pool.wait_ge(stats_done, i + 1)
                nc.gpsimd.tensor_tensor(vareps[:, :], mv[:, :, 1], epsv[:, :], ALU.add).then_inc(vareps_done, 1)
                pool.wait_ge(vareps_done, i + 1)
                nc.gpsimd.tensor_tensor(rstd[:, :], vareps[:, :], npow[:, :], ALU.pow).then_inc(rstd_done, 1)

            def residual(i):
                pool.wait_ge(x_loaded, 16 * (i + 1))
                nc.gpsimd.tensor_tensor(y[:, ds(i * BT, BT), :], x_in[:, :, :],
                                        bo_sb[:, :].unsqueeze(1).broadcast_to([P, BT, D]),
                                        ALU.add).then_inc(ybase_done, 1)

            def split(i, first, last):
                for t in range(BT):
                    if t == 3 and not last:
                        norm_scale(i + 1)
                    pool.wait_ge(rest_done, BT * i + t + 1)
                    cols = slice(t * P, (t + 1) * P)
                    r = rest[t % 2][:, :].rearrange("p (a n) -> p a n", a=3)
                    nc.gpsimd.tensor_tensor(qkp[:, 1, :, cols], r, zeros[:, :].unsqueeze(2).broadcast_to([P, 3, P]), ALU.add).then_inc(part2_done, 1)
                    pool.wait_ge(part2_done, BT * i + t + 1)
                    nc.gpsimd.tensor_tensor(qkp[:, 2, :, cols], r, qkp[:, 1, :, cols],
                                            ALU.subtract).then_inc(part3_done, 1)
                if not last:
                    residual(i + 1)

            pool.wait_ge(consts_set, N_CONSTS)
            norm_scale(0)
            for n in range(2):
                cols = slice(n * HID // 2, (n + 1) * HID // 2)
                pool.wait_ge(w13_hi, 2 * n + 2)
                nc.gpsimd.tensor_tensor(w3_p[1][:, :, cols], w13_raw[:, 1, :, cols],
                                        w3_p[0][:, :, cols].bitcast(F32), ALU.subtract).then_inc(w3_lo, 1)
            pool.wait_ge(bo_in, 16)
            residual(0)
            for stage in range(FWHT_STAGES - 1):
                transform(pool, nc.gpsimd, stage)
            split(0, True, False)
            with pool.Fori(1, NBLK - 1) as i:
                split(i, False, False)
            split(NBLK - 1, False, True)

            def split_max(p, k, n, free):
                pool.wait_ge(ring_free, free)
                m = negmax[p][:, 2 * k:2 * k + 2, :]
                to = [mparts[p][:, c, 2 * k:2 * k + 2, :] for c in range(MROWS)]
                nc.gpsimd.tensor_tensor(to[0], m, zeros[:, :].unsqueeze(2).broadcast_to([P, 2, ST]), ALU.add).then_inc(m_part1, 1)
                pool.wait_ge(m_part1, n + 1)
                nc.gpsimd.tensor_tensor(mrest[k][:, :, :], m, to[0], ALU.subtract).then_inc(m_rest, 1)
                pool.wait_ge(m_rest, n + 1)
                nc.gpsimd.tensor_tensor(to[1], mrest[k][:, :, :], zeros[:, :].unsqueeze(2).broadcast_to([P, 2, ST]), ALU.add).then_inc(m_part2, 1)
                pool.wait_ge(m_part2, n + 1)
                nc.gpsimd.tensor_tensor(to[2], mrest[k][:, :, :], to[1],
                                        ALU.subtract).then_inc(m_split, 1)

            def normalise_sums(i, half):
                pool.wait_ge(moved[half], N_MOVE * 2 * i)
                nc.gpsimd.tensor_tensor(attnt[:, half, :], attnt[:, half, :], recips[:, half, :],
                                        ALU.mult).then_inc(norm_done, 1)

            done = 0
            for g in range(LEAD):
                done += 2
                if g % ST == ST - 1:
                    split_max(g // STEPS, (g % STEPS) // ST, g // ST, done)
                done = done + len(lead_entries(g)) - 2

            def iteration(i, first, last):
                n = 0
                for now in ring_schedule(first, last):
                    for kind, q, unit in now:
                        n += kind in RING
                        if kind == "NM":
                            normalise_sums(i, q)
                        if kind == "S1" and unit % (2 * ST) == 2 * ST - 1:
                            k = unit // (2 * ST)
                            split_max(q % 2, k, 4 * i + 2 * q + k, ring_base(i) + n)

            iteration(0, True, False)
            with pool.Fori(1, NIT - 1) as i:
                iteration(i, False, False)
            iteration(NIT - 1, False, True)
            for half in range(QB):
                normalise_sums(NIT, half)

        @block.scalar
        def _(act):
            act.dma_start(wqkv_raw, wqkv.rearrange("(c p) n -> p c n", p=P)).then_inc(wqkv_in, 16)
            act.dma_start(bqkv_sb[:, :], bqkv.partition_broadcast(P)).then_inc(tables_in, 16)
            for t, src in ((cos_sb, cos_t), (sin_sb, sin_t), (nsin_sb, nsin_t)):
                act.dma_start(t[:, :, :], src.rearrange("(t p) f -> p t f", p=P)).then_inc(tables_in, 16)
            act.dma_start(bo_sb[:, :], bo.partition_broadcast(P)).then_inc(bo_in, 16)
            act.dma_start(w2h[0][:, :, :], w2t.rearrange("(c p) n -> p c n", p=P)).then_inc(w2_in, 16)
            act.dma_start(had[:, :], had_in).then_inc(w2_in, 16)

            act.wait_ge(id_in, 16)
            nc.scalar.copy(identb[:, :], ident[:, :]).then_inc(identb_done, 1)
            act.wait_ge(wqkv_in, 16)
            nc.scalar.copy(wqkv_p[0][:, :, :], wqkv_raw).then_inc(wqkv_hi, 1)

            def turned_hi(i):
                for k in range(DC):
                    act.wait_ge(xt_done, DC * i + k + 1)
                    nc.scalar.copy(xnt_p[0][:, k, :], ps[:, 6 + k, :]).then_inc(xnt_hi, 1)

            def hidden_hi(i, c, first):
                act.wait_ge(hid_done, HC * i + c + 1)
                if c == 0 and not first:
                    act.wait_ge(down_done, BT * i)
                nc.scalar.copy(hid_p[0][:, c, :], sg[c % 2][:, :]).then_inc(hid_hi, 1)

            def stage1(i, first, last):
                for c in range(HC):
                    if first and c == HC - 1:
                        for n in range(4):
                            act.wait_ge(w2t_done, n + 1)
                            nc.scalar.copy(w2t_p[0][:, 2 * n:2 * n + 2, :],
                                           ps[:, 4 + n, :].rearrange("p (c d) -> p c d", c=2)).then_inc(w2t_hi, 1)
                    act.wait_ge(gate_done, HC * i + c + 1)
                    if not (first and c < 2):
                        act.wait_ge(hid_lo, HC * i + c - 1)
                    nc.scalar.activation(sg[c % 2][:, :], ps[:, c % 2, :], ACT.Silu).then_inc(silu_done, 1)
                    if c > 0:
                        hidden_hi(i, c - 1, first)
                    t = c - 2
                    if 0 <= t < BT:
                        if t == 0 and not first:
                            act.wait_ge(parts_out, 16 * 3 * i)
                        act.wait_ge(qt_done, BT * i + t + 1)
                        nc.scalar.copy(qkp[:, 0, :, t * P:(t + 1) * P],
                                       ps[:, 4 + t, 0:QKP].rearrange("p (a n) -> p a n", a=3)).then_inc(part1_done, 1)
                hidden_hi(i, HC - 1, first)
                if not last:
                    turned_hi(i + 1)

            turned_hi(0)
            for n in range(2):
                cols = slice(n * HID // 2, (n + 1) * HID // 2)
                act.wait_ge(w13_in[n], 32)
                for w, to in enumerate((w1_p, w3_p)):
                    nc.scalar.copy(to[0][:, :, cols], w13_raw[:, w, :, cols]).then_inc(w13_hi, 1)
            stage1(0, True, False)
            with act.Fori(1, NBLK - 1) as i:
                stage1(i, False, False)
            stage1(NBLK - 1, False, True)

            def save_sums(i, s):
                if s == -1:
                    i, s = i - 1, ITSTEPS - 1
                k = (s + 1) // ST
                act.wait_ge(pv_done, ITSTEPS * i + s + 1)
                if not (isinstance(i, int) and i == 0 and k == 1):
                    act.wait_ge(moved[k % 2], N_MOVE * (2 * i + k // 2))
                nc.scalar.copy(osum[:, :], ps[:, 7, :]).then_inc(osum_done, 1)

            def iteration(i, first, last):
                for j in range(ITSTEPS):
                    for h in range(QUAD):
                        if h == 1 and j % ST == 1 and not (first and j == 1):
                            save_sums(i, j - 2)
                        u = QUAD * j + h
                        act.wait_ge(s2_done, QUAD * ITSTEPS * i + u + 1)
                        if h == 0 and not (first and j < 2):
                            act.wait_ge(pv_done, ITSTEPS * i + j - 1)
                        nc.scalar.activation(prob[j % 2][:, h, :], ps[:, 4 + u % 3, :], ACT.Exp,
                                             scale=SCALE).then_inc(exp_done, 1)

            iteration(0, True, False)
            with act.Fori(1, NIT - 1) as i:
                iteration(i, False, False)
            iteration(NIT - 1, False, True)
            save_sums(NIT - 1, ITSTEPS - 1)

        @block.vector
        def _(dve):
            def norm_stats(i):
                dve.wait_ge(x_loaded, 16 * (i + 1))
                for t in range(BT):
                    nc.vector.bn_stats(stats[:, t, :], x_in[:, t, :]).then_inc(stats_part, 1)

            def gather_stats(i):
                for t in range(BT):
                    a = nc.vector.bn_aggr(mv[:, t, :], stats[:, t, :])
                a.then_inc(stats_done, 1)

            def normalise(i):
                dve.wait_ge(stats_done, i + 1)
                dve.wait_ge(rstd_done, i + 1)
                for t in range(BT):
                    a = nc.vector.tensor_scalar(xn[:, t, :], x_in[:, t, :], mv[:, t, 0:1], rstd[:, t:t + 1],
                                                ALU.subtract, ALU.mult)
                a.then_inc(xn_done, 1)

            def rotate(i, t):
                n = BT * i + t
                tile = ds(n, 1)
                bank = ps[:, 4 + t, :]
                dve.wait_ge(qkv_done, n + 1)
                if not (isinstance(n, int) and n < 2):
                    dve.wait_ge(qt_done, n - 1)
                nc.vector.tensor_tensor(biased[:, :], bank[:, 0:RQK], bqkv_sb[:, 0:RQK], ALU.add).then_inc(rope_step, 1)
                nc.vector.tensor_tensor(
                    v_all[:, tile, :, :].rearrange("p a g d -> p (a g) d"),
                    bank[:, RQK:QKV].rearrange("p (g d) -> p g d", g=NG),
                    bqkv_sb[:, RQK:QKV].rearrange("p (g d) -> p g d", g=NG), ALU.add).then_inc(rope_step, 1)
                dve.wait_ge(rope_step, 5 * n + 2)
                if not (isinstance(n, int) and n == 0):
                    dve.wait_ge(rope_done, n)
                at = ds((i % 2) * BT + t, 1)
                v = biased[:, :].rearrange("p (h s f) -> p h s f", s=2, f=HALF)
                vc = rcos[:, :].rearrange("p (h s f) -> p h s f", s=2, f=HALF)
                vs = rsin[:, :].rearrange("p (h s f) -> p h s f", s=2, f=HALF)
                nc.vector.tensor_tensor(vc, v, cos_sb[:, at, :].unsqueeze(1).broadcast_to([P, NH + NG, 2, HALF]),
                                        ALU.mult).then_inc(rope_step, 1)
                nc.vector.tensor_tensor(vs[:, :, 0, :], v[:, :, 1, :],
                                        nsin_sb[:, at, :].broadcast_to([P, NH + NG, HALF]),
                                        ALU.mult).then_inc(rope_step, 1)
                nc.vector.tensor_tensor(vs[:, :, 1, :], v[:, :, 0, :],
                                        sin_sb[:, at, :].broadcast_to([P, NH + NG, HALF]),
                                        ALU.mult).then_inc(rope_step, 1)
                dve.wait_ge(rope_step, 5 * n + 5)
                nc.vector.tensor_tensor(roped[t % 2][:, 0:RQK], rcos[:, :], rsin[:, :], ALU.add).then_inc(rope_done, 1)

            def split_rest(i, t):
                dve.wait_ge(part1_done, BT * i + t + 1)
                if not (isinstance(i, int) and i == 0 and t < 2):
                    dve.wait_ge(part3_done, BT * i + t - 1)
                nc.vector.tensor_tensor(rest[t % 2][:, :].rearrange("p (a n) -> p a n", a=3),
                                        ps[:, 4 + t, 0:QKP].rearrange("p (a n) -> p a n", a=3),
                                        qkp[:, 0, :, t * P:(t + 1) * P], ALU.subtract).then_inc(rest_done, 1)

            def hidden(i, c):
                dve.wait_ge(silu_done, HC * i + c + 1)
                dve.wait_ge(lin_done, HC * i + c + 1)
                nc.vector.tensor_tensor(sg[c % 2][:, :], sg[c % 2][:, :], ps[:, 2 + c % 2, :],
                                        ALU.mult).then_inc(hid_done, 1)

            def hidden_lo(i, c):
                dve.wait_ge(hid_hi, HC * i + c + 1)
                nc.vector.tensor_tensor(hid_p[1][:, c, :], sg[c % 2][:, :], hid_p[0][:, c, :].bitcast(F32),
                                        ALU.subtract).then_inc(hid_lo, 1)

            def turned_lo(i):
                for k in range(DC):
                    dve.wait_ge(xnt_hi, DC * i + k + 1)
                    nc.vector.tensor_tensor(xnt_p[1][:, k, :], ps[:, 6 + k, :], xnt_p[0][:, k, :].bitcast(F32),
                                            ALU.subtract).then_inc(xnt_lo, 1)

            def stage1(i, first, last):
                rotate(i, 0)
                rotate(i, 1)
                for c in range(HC):
                    if first and c == HC - 1:
                        for n in range(4):
                            dve.wait_ge(w2t_hi, n + 1)
                            nc.vector.tensor_tensor(
                                w2t_p[1][:, 2 * n:2 * n + 2, :].rearrange("p c d -> p (c d)"), ps[:, 4 + n, :],
                                w2t_p[0][:, 2 * n:2 * n + 2, :].bitcast(F32).rearrange("p c d -> p (c d)"),
                                ALU.subtract).then_inc(w2t_lo, 1)
                    if c == 3 and not last:
                        dve.wait_ge(stats_part, BT * (i + 2))
                    hidden(i, c)
                    if c == 3 and not last:
                        gather_stats(i + 1)
                    if c > 0:
                        hidden_lo(i, c - 1)
                    if c < 2:
                        rotate(i, c + 2)
                    elif c < 2 + BT:
                        split_rest(i, c - 2)
                    if first and c == 5:
                        transform(dve, nc.vector, FWHT_STAGES - 1)
                    if c == 2 and not last:
                        norm_stats(i + 1)
                    if c == 6 and not last:
                        normalise(i + 1)
                hidden_lo(i, HC - 1)
                if not last:
                    turned_lo(i + 1)
                for t in range(BT):
                    dve.wait_ge(down_done, BT * i + t + 1)
                    if t == 0:
                        dve.wait_ge(ybase_done, i + 1)
                    at = y[:, ds(BT * i + t, 1), :].rearrange("p a d -> p (a d)")
                    nc.vector.tensor_tensor(at, at, ps[:, t, 0:D], ALU.add).then_inc(y_done, 1)

            norm_stats(0)
            dve.wait_ge(stats_part, BT)
            gather_stats(0)
            dve.wait_ge(consts_set, N_CONSTS)
            normalise(0)
            dve.wait_ge(wqkv_hi, 1)
            nc.vector.tensor_tensor(wqkv_p[1][:, :, :], wqkv_raw, wqkv_p[0][:, :, :].bitcast(F32),
                                    ALU.subtract).then_inc(wqkv_lo, 1)
            turned_lo(0)
            for n in range(2):
                cols = slice(n * HID // 2, (n + 1) * HID // 2)
                dve.wait_ge(w13_hi, 2 * n + 1)
                nc.vector.tensor_tensor(w1_p[1][:, :, cols], w13_raw[:, 0, :, cols],
                                        w1_p[0][:, :, cols].bitcast(F32), ALU.subtract).then_inc(w1_lo, 1)
            dve.wait_ge(tables_in, 16 * 4)
            stage1(0, True, False)
            with dve.Fori(1, NBLK - 1) as i:
                stage1(i, False, False)
            stage1(NBLK - 1, False, True)

            def consume(entry, i, n, slot, first):
                kind, a, b = entry
                two = pair(slot)
                if kind in RING:
                    dve.wait_ge(ring_full, n + 1)
                if kind == "RC":
                    m = 4 * i + (a + 1) % 4
                    dve.wait_ge(dens_in, 16 * QUAD * m)
                    nc.vector.reciprocal(dens[:, :], dens[:, :]).then_inc(recip_done, 1)
                if kind == "CV":
                    if a == 1:
                        if not first:
                            dve.wait_ge(pv_done, ITSTEPS * i)
                        copy_values(i, 1)
                    else:
                        dve.wait_ge(pv_done, ITSTEPS * i + STEPS)
                        copy_values(i + 1, 0)
                if kind == "S1":
                    h, t = b // ST, b % ST
                    if b == 0 and not (first and a < 2):
                        dve.wait_ge(m_split, 4 * i + 2 * (a - 1))
                    nc.vector.tensor_reduce(negmax[a % 2][:, h, t:t + 1], two, AX.XY, ALU.max,
                                            negate=True).then_inc(ring_free, 1)
                if kind == "MT":
                    if not (first and a < 2):
                        dve.wait_ge(mrows_in[a % 2], 16 * MROWS * (i + a // 2))
                    nc.vector.tensor_copy(mturned[a % 2][:, :], turned_maxima(two)).then_inc(mturned_done, 1)
                    nc.vector.engine_nop().then_inc(ring_free, 1)
                if kind == "WO":
                    at = y[:, ds(((i - 1) % B) * ST + 4 * a, 4), :].rearrange("p t d -> p (t d)")
                    nc.vector.tensor_tensor(at, at, two.rearrange("p a n -> p (a n)"), ALU.add).then_inc(ring_free, 1)

            def copy_values(i, p):
                g, b = i // B, i % B
                nc.vector.tensor_scalar(
                    v2[p][:, :, 0:HD],
                    v_all[:, ds(b * ST, ST), ds(g, 1), :].rearrange("p t a v -> p (t a) v"),
                    1.0, None, ALU.mult).then_inc(v2_done, 1)

            n = 0
            copy_values(0, 0)
            for g in range(LEAD):
                for entry in lead_entries(g):
                    consume(entry, 0, n, n % 2, True)
                    n += 1

            def iteration(i, first, last):
                n = 0
                for now in ring_schedule(first, last):
                    for entry in now:
                        consume(entry, i, ring_base(i) + n, ring_parity(i, n), first)
                        n += entry[0] in RING
                return n

            iteration(0, True, False)
            with dve.Fori(1, NIT - 1) as i:
                iteration(i, False, False)
            n = iteration(NIT - 1, False, True)
            for entry in TAIL:
                consume(entry, NIT, ring_base(NIT - 1) + n, ring_parity(NIT - 1, n), False)
                n += entry[0] in RING

        @block.tensor
        def _(pe):
            def product(out, left, right, first, last):
                for n, (a, b) in enumerate(((0, 0), (0, 1), (1, 0))):
                    m = pe.matmul(out, left[a], right[b], start=(first and n == 0), stop=(last and n == 2))
                return m

            def turn(i, first):
                pe.wait_ge(xn_done, i + 1)
                if not first:
                    pe.wait_ge(rest_done, BT * i)
                for c in range(DC):
                    for t in range(BT):
                        a = pe.transpose(ps[:, 6 + c, t * P:(t + 1) * P], xn[:, t, c * P:(c + 1) * P], ident[:, :])
                    a.then_inc(xt_done, 1)

            def stage1(i, first, last):
                pe.wait_ge(xnt_lo, DC * (i + 1))
                for t in range(BT):
                    for c in range(DC):
                        a = product(ps[:, 4 + t, 0:QKV], [x[:, c, t * P:(t + 1) * P] for x in xnt_p],
                                    [w[:, c, :] for w in wqkv_p], c == 0, c == DC - 1)
                    a.then_inc(qkv_done, 1)
                for c in range(HC):
                    if c < 2:
                        if not first:
                            pe.wait_ge(y_done, BT * i)
                    else:
                        pe.wait_ge(hid_done, HC * i + c - 1)
                    if first and c == HC - 1:
                        pe.wait_ge(w2_in, 32)
                        pe.wait_ge(fwht_step, 2 * FWHT_STAGES)
                        pe.wait_ge(rest_done, BT)
                        for n in range(4):
                            for m in range(2):
                                a = pe.matmul(ps[:, 4 + n, m * D:(m + 1) * D], had[:, :],
                                              w2h[FWHT_STAGES % 2][:, 2 * n + m, :], start=True, stop=True)
                            a.then_inc(w2t_done, 1)
                    if first and c % (HC // 2) == 0:
                        pe.wait_ge(w1_lo, c // (HC // 2) + 1)
                        pe.wait_ge(w3_lo, c // (HC // 2) + 1)
                    for w, bank, done in ((w1_p, c % 2, gate_done), (w3_p, 2 + c % 2, lin_done)):
                        for k in range(DC):
                            a = product(ps[:, bank, :], [v[:, k, c * P:(c + 1) * P] for v in w],
                                        [x[:, k, :] for x in xnt_p], k == 0, k == DC - 1)
                        a.then_inc(done, 1)
                    t = c - 1
                    if 0 <= t < BT:
                        pe.wait_ge(rope_done, BT * i + t + 1)
                        for k in range(3):
                            a = pe.transpose(ps[:, 4 + t, k * P:(k + 1) * P], roped[t % 2][:, k * P:(k + 1) * P],
                                             ident[:, :])
                        a.then_inc(qt_done, 1)
                if first:
                    pe.wait_ge(w2t_lo, 4)
                if not last:
                    turn(i + 1, False)
                for t in range(BT):
                    for c in range(HC):
                        if t == 0 and c in (0, HC - 1):
                            pe.wait_ge(hid_lo, HC * i + HC - (1 if c == 0 else 0))
                        a = product(ps[:, t, 0:D], [h[:, c, t * P:(t + 1) * P] for h in hid_p],
                                    [w[:, c, :] for w in w2t_p], c == 0, c == HC - 1)
                    a.then_inc(down_done, 1)

            pe.wait_ge(id_in, 16)
            turn(0, True)
            pe.wait_ge(wqkv_lo, 1)
            stage1(0, True, False)
            with pe.Fori(1, NBLK - 1) as i:
                stage1(i, False, False)
            stage1(NBLK - 1, False, True)
            pe.wait_ge(identb_done, 1)
            pe.wait_ge(wo_in, 16)

            pe.wait_ge(y_done, NTILE)
            pe.wait_ge(rest_done, NTILE)

            def fill(entry, i, n, slot, first):
                kind, a, b = entry
                if kind not in RING:
                    return
                two = pair(slot)
                if not (isinstance(n, int) and n < 2):
                    pe.wait_ge(ring_free, n - 1)
                if kind == "S1":
                    p, h, t = a % 2, b // ST, b % ST
                    if b == 0:
                        pe.wait_ge(in1[p], N_IN * (i + a // 2 + 1))
                    for e in range(2):
                        m = pe.matmul(two[:, e, :], q1[p][:, h, t * P:(t + 1) * P], k1[p][:, e * 512:(e + 1) * 512],
                                      start=True, stop=True)
                if kind == "MT":
                    pe.wait_ge(m_split, 4 * i + 2 * a + 2)
                    m = pe.transpose(turned_maxima(two), mparts[a % 2][:, :, :, :].rearrange("p c h t -> p (c h t)"),
                                     identb[:, :])
                if kind == "WO":
                    g = (i - 1) // B
                    pe.wait_ge(norm_done, 2 * (i - 1) + a + 1)
                    for t in range(4):
                        m = pe.matmul(two[:, t // 2, (t % 2) * D:(t % 2 + 1) * D],
                                      attnt[:, a, t * P:(t + 1) * P],
                                      wo_sb[:, ds(g, 1), :].rearrange("p a n -> p (a n)"), start=True, stop=True)
                m.then_inc(ring_full, 1)

            n = 0
            for g in range(LEAD):
                for entry in lead_entries(g):
                    fill(entry, 0, n, n % 2, True)
                    n += 1

            def scores(i, first, j, h):
                u = QUAD * j + h
                p, half, kt = j // STEPS, (j % STEPS) // ST, j % ST
                if j % STEPS == 0 and h == 0:
                    pe.wait_ge(in2[p], N_IN * (i + 1))
                    pe.wait_ge(mrows_in[p], 16 * MROWS * (i + 1))
                before = u - 3 if u >= 3 else {0: -2, 1: -1, 2: -3}[u]
                if not (first and before < 0):
                    pe.wait_ge(exp_done, QUAD * ITSTEPS * i + before + 1)
                pe.matmul(ps[:, 4 + u % 3, :], k2[p][:, kt * P:(kt + 1) * P], q2[p][:, h, half * 512:(half + 1) * 512],
                          start=True, stop=True).then_inc(s2_done, 1)

            def sums(i, first, s):
                p, kt = s // STEPS, s % ST
                if s % STEPS == 0:
                    pe.wait_ge(v2_done, 2 * i + p + 1)
                if kt == 0 and not (first and s == 0):
                    pe.wait_ge(osum_done, 4 * i + s // ST)
                pe.wait_ge(exp_done, QUAD * ITSTEPS * i + QUAD * (s + 1))
                for h in range(QUAD):
                    m = pe.matmul(ps[VW * h:VW * (h + 1), 7, :], v2[p][:, kt, :], prob[s % 2][:, h, :],
                                  start=(kt == 0), stop=(kt == ST - 1))
                m.then_inc(pv_done, 1)

            def iteration(i, first, last):
                n = 0
                for place, now in enumerate(ring_schedule(first, last)):
                    j, k = place // GAPS, place % GAPS
                    if k != SUMS_AT:
                        scores(i, first, j, k if k < SUMS_AT else k - 1)
                    elif j > 0:
                        sums(i, first, j - 1)
                    elif not first:
                        sums(i - 1, False, ITSTEPS - 1)
                    for entry in now:
                        fill(entry, i, ring_base(i) + n, ring_parity(i, n), first)
                        n += entry[0] in RING
                return n

            iteration(0, True, False)
            with pe.Fori(1, NIT - 1) as i:
                iteration(i, False, False)
            n = iteration(NIT - 1, False, True)
            for entry in TAIL:
                fill(entry, NIT, ring_base(NIT - 1) + n, ring_parity(NIT - 1, n), False)
                n += entry[0] in RING
                if entry == ("WO", 0, 0):
                    sums(NIT - 1, False, ITSTEPS - 1)


def kernel(**inputs):
    import numpy as np
    import concourse.bacc as bacc
    from concourse.bass_utils import run_bass_kernel_spmd

    a = {k: np.asarray(v) for k, v in inputs.items()}
    inv_freq = (1.0 / np.float32(1250) ** (np.arange(0, HD, 2, dtype=np.float32) / np.float32(HD))).astype(np.float32)
    freqs = np.outer(np.arange(S, dtype=np.float32), inv_freq).astype(np.float32)
    sin = np.sin(freqs).astype(np.float32)
    hadamard = np.ones((1, 1))
    while hadamard.shape[0] < P:
        hadamard = np.kron(np.array([[1, 1], [1, -1]]), hadamard)
    hadamard = hadamard / np.sqrt(HID)
    arrays = {
        "x": a["L0_attn_x"],
        "wqkv": np.concatenate([a["L0_attn_wq"], a["L0_attn_wk"], a["L0_attn_wv"]], axis=1),
        "bqkv": np.concatenate([a["L0_attn_bq"], a["L0_attn_bk"], a["L0_attn_bv"]]),
        "wo": a["L0_attn_wo"],
        "bo": a["L0_attn_bo"],
        "w1t": a["L0_ffn_W1"].T,
        "w3t": a["L0_ffn_W3"].T,
        "w2t": a["L0_ffn_W2"].T,
        "cos_t": np.cos(freqs).astype(np.float32),
        "sin_t": sin,
        "nsin_t": -sin,
        "ident_in": np.eye(P, dtype=np.float32),
        "had_in": hadamard.astype(np.float32),
    }
    nc = bacc.Bacc("TRN2", target_bir_lowering=False, num_devices=1)
    feed, aps = {}, {}
    for name, v in arrays.items():
        v = np.ascontiguousarray(v)
        feed[f"in_{name}"] = v
        aps[name] = nc.dram_tensor(f"in_{name}", v.shape, mybir.dt.from_np(v.dtype), kind="ExternalInput").ap()
    out = nc.dram_tensor("out", (B, S, D), F32, kind="ExternalOutput").ap()
    build(nc, *aps.values(), out)
    r = run_bass_kernel_spmd(nc, [feed], core_ids=[0])
    return r.results[0]["out"]
```
